# Optimizing a Trainium2 kernel written in Bass

```python
import numpy as np
import jax
import jax.numpy as jnp

def _softmax(x, axis=-1):
    return jax.nn.softmax(x, axis=axis)

def _gelu(x):
    return jax.nn.gelu(x, approximate=True)

def _silu(x):
    return jax.nn.silu(x)

def _sigmoid(x):
    return jax.nn.sigmoid(x)

def _layernorm(x, axis=-1, eps=1e-05):
    m = jnp.mean(x, axis=axis, keepdims=True)
    v = jnp.var(x, axis=axis, keepdims=True)
    return (x - m) / jnp.sqrt(v + eps)

def _scatter_add(tgt, idx, src, axis=0):
    return tgt.at[idx].add(src)

def _segment_sum(src, seg, n):
    return jax.ops.segment_sum(src, seg, n)
kernel_name = 'mk_prb_d1_jaxref_r8_a3f553'

def setup_inputs(seed: int=0):
    np.random.seed(seed)
    _w = jnp.asarray

    def _L0_attn_setup():
        import jax, jax.numpy as jnp
        import numpy as np
        HEADS = 16
        NUM_LANDMARKS = 64
        PINV_ITERS = 6
        D_MODEL = 128

        def _moore_penrose_pinv(x, num_iters):
            m = x.shape[-1]
            I = jnp.eye(m, dtype=x.dtype)
            V = x
            for _ in range(num_iters):
                KV = x @ V
                V = 0.25 * V @ (13.0 * I - KV @ (15.0 * I - KV @ (7.0 * I - KV)))
            return V
        key = jax.random.key(seed)
        k1, k2, k3 = jax.random.split(key, 3)
        b, n, d = (4, 512, D_MODEL)
        hidden_states = jax.random.normal(k1, (b, n, d), dtype=jnp.float32)
        Wqkv = jax.random.normal(k2, (d, 3 * d), dtype=jnp.float32) * 0.02
        bqkv = jnp.zeros((3 * d,), dtype=jnp.float32)
        Wout = jax.random.normal(k3, (d, d), dtype=jnp.float32) * 0.02
        bout = jnp.zeros((d,), dtype=jnp.float32)
        return {'hidden_states': hidden_states, 'Wqkv': Wqkv, 'bqkv': bqkv, 'Wout': Wout, 'bout': bout}
    _L0_attn_in = _L0_attn_setup()

    def _L0_ffn_setup():
        import jax, jax.numpy as jnp
        import numpy as np
        DIM = 128
        DEPTH = 6
        HEADS = 16
        DIM_HEAD = 64
        WINDOW = 32
        INNER = HEADS * DIM_HEAD
        DIM_INNER = int(DIM * 4 * 2 / 3)
        QK_SCALE = 8.0

        def shift_tokens(t):
            a, s = jnp.split(t, 2, -1)
            s = jnp.pad(s, ((0, 0), (1, 0), (0, 0)))[:, :-1]
            return jnp.concatenate([a, s], -1)

        def l2norm(t):
            return t / jnp.maximum(jnp.linalg.norm(t, axis=-1, keepdims=True), 1e-12)

        def rotate_half(x):
            x1, x2 = jnp.split(x, 2, -1)
            return jnp.concatenate([-x2, x1], -1)

        def rotary_tables(n):
            half = jnp.arange(0, DIM_HEAD, 2, dtype=jnp.float32)
            inv_freq = 1.0 / 10000.0 ** (half / DIM_HEAD)
            t = jnp.arange(n, dtype=jnp.float32)
            freqs = t[:, None] * inv_freq[None, :]
            freqs = jnp.concatenate([freqs, freqs], -1)
            base_scale = (half + 0.4 * DIM_HEAD) / (1.4 * DIM_HEAD)
            power = (t - n // 2) / (WINDOW // 2)
            scale = base_scale[None, :] ** power[:, None]
            scale = jnp.concatenate([scale, scale], -1)
            return (freqs, scale)

        def local_attention(q, k, v):
            b, h, n, d = q.shape
            w = WINDOW
            nw = n // w
            bq = q.reshape(b, h, nw, w, d)
            bk = k.reshape(b, h, nw, w, d)
            bv = v.reshape(b, h, nw, w, d)

            def look(t):
                p = jnp.pad(t, ((0, 0), (0, 0), (1, 0), (0, 0), (0, 0)))
                return jnp.concatenate([p[:, :, :nw], p[:, :, 1:]], axis=3)
            bk2, bv2 = (look(bk), look(bv))
            seq = jnp.arange(n).reshape(nw, w)
            seq_p = jnp.pad(seq, ((1, 0), (0, 0)), constant_values=-1)
            jt = jnp.concatenate([seq_p[:nw], seq_p[1:]], axis=1)
            it = seq[:, :, None]
            jb = jt[:, None, :]
            mask = (it < jb) | (it > jb + w) | (jb == -1)
            sim = jnp.einsum('bhwie,bhwje->bhwij', bq, bk2) * QK_SCALE
            sim = jnp.where(mask, -jnp.finfo(sim.dtype).max, sim)
            attn = jax.nn.softmax(sim, -1)
            out = jnp.einsum('bhwij,bhwje->bhwie', attn, bv2)
            return out.reshape(b, h, n, d)

        def attn_layer(x, Wqkv, qs, ksc, Wo):
            b, n, _ = x.shape
            qkv = x @ Wqkv
            q, k, v = jnp.split(qkv, 3, -1)
            sh = lambda t: t.reshape(b, n, HEADS, DIM_HEAD).transpose(0, 2, 1, 3)
            q, k, v = (sh(q), sh(k), sh(v))
            q = l2norm(q) * qs
            k = l2norm(k) * ksc
            freqs, scale = rotary_tables(n)
            cos, sin = (jnp.cos(freqs), jnp.sin(freqs))
            q = q * cos * scale + rotate_half(q) * sin * scale
            inv = 1.0 / scale
            k = k * cos * inv + rotate_half(k) * sin * inv
            out = local_attention(q, k, v)
            out = out.transpose(0, 2, 1, 3).reshape(b, n, INNER)
            return out @ Wo

        def ffn_layer(x, g, bln, W1, b1, W2, b2):
            mu = x.mean(-1, keepdims=True)
            var = ((x - mu) ** 2).mean(-1, keepdims=True)
            xn = (x - mu) / jnp.sqrt(var + 1e-05) * g + bln
            hg = xn @ W1 + b1
            a, gate = jnp.split(hg, 2, -1)
            return a * jax.nn.gelu(gate, approximate=False) @ W2 + b2
        key = jax.random.key(seed)
        ks = jax.random.split(key, 8)
        B, N = (2, 256)
        init = lambda k, shape: jax.random.normal(k, shape, jnp.float32) * 0.02
        return {'x': jax.random.normal(ks[0], (B, N, DIM), jnp.float32), 'Wqkv': init(ks[1], (DEPTH, DIM, 3 * INNER)), 'q_scale': jnp.ones((DEPTH, DIM_HEAD), jnp.float32), 'k_scale': jnp.ones((DEPTH, DIM_HEAD), jnp.float32), 'Wo': init(ks[2], (DEPTH, INNER, DIM)), 'ln_g': jnp.ones((DEPTH, DIM), jnp.float32), 'ln_b': jnp.zeros((DEPTH, DIM), jnp.float32), 'W1': init(ks[3], (DEPTH, DIM, 2 * DIM_INNER)), 'b1': jnp.zeros((DEPTH, 2 * DIM_INNER), jnp.float32), 'W2': init(ks[4], (DEPTH, DIM_INNER, DIM)), 'b2': jnp.zeros((DEPTH, DIM), jnp.float32)}
    _L0_ffn_in = _L0_ffn_setup()
    _d = {'L0_attn_hidden_states': _L0_attn_in['hidden_states'], 'L0_attn_Wqkv': _L0_attn_in['Wqkv'], 'L0_attn_bqkv': _L0_attn_in['bqkv'], 'L0_attn_Wout': _L0_attn_in['Wout'], 'L0_attn_bout': _L0_attn_in['bout'], 'L0_ffn_Wqkv': _L0_ffn_in['Wqkv'], 'L0_ffn_q_scale': _L0_ffn_in['q_scale'], 'L0_ffn_k_scale': _L0_ffn_in['k_scale'], 'L0_ffn_Wo': _L0_ffn_in['Wo'], 'L0_ffn_ln_g': _L0_ffn_in['ln_g'], 'L0_ffn_ln_b': _L0_ffn_in['ln_b'], 'L0_ffn_W1': _L0_ffn_in['W1'], 'L0_ffn_b1': _L0_ffn_in['b1'], 'L0_ffn_W2': _L0_ffn_in['W2'], 'L0_ffn_b2': _L0_ffn_in['b2']}
    _x0 = _d['L0_attn_hidden_states']
    _d['L0_attn_hidden_states'] = jax.random.normal(jax.random.fold_in(jax.random.key(seed), 1), (2, 2048, 128), dtype=_x0.dtype)
    del _x0
    return _d

def reference(L0_attn_hidden_states, L0_attn_Wqkv, L0_attn_bqkv, L0_attn_Wout, L0_attn_bout, L0_ffn_Wqkv, L0_ffn_q_scale, L0_ffn_k_scale, L0_ffn_Wo, L0_ffn_ln_g, L0_ffn_ln_b, L0_ffn_W1, L0_ffn_b1, L0_ffn_W2, L0_ffn_b2):

    def _L0_attn_ref(hidden_states, Wqkv, bqkv, Wout, bout):
        import jax, jax.numpy as jnp
        import numpy as np
        HEADS = 16
        NUM_LANDMARKS = 64
        PINV_ITERS = 6
        D_MODEL = 128

        def _moore_penrose_pinv(x, num_iters):
            m = x.shape[-1]
            I = jnp.eye(m, dtype=x.dtype)
            V = x
            for _ in range(num_iters):
                KV = x @ V
                V = 0.25 * V @ (13.0 * I - KV @ (15.0 * I - KV @ (7.0 * I - KV)))
            return V
        b, n, d = hidden_states.shape
        h, m = (HEADS, NUM_LANDMARKS)
        dh = d // h
        scale = 1.0 / np.sqrt(dh).astype(np.float32)
        l = n // m
        qkv = hidden_states @ Wqkv + bqkv
        q, k, v = jnp.split(qkv, 3, axis=-1)

        def to_heads(t):
            return t.reshape(b, n, h, dh).transpose(0, 2, 1, 3)
        q, k, v = (to_heads(q), to_heads(k), to_heads(v))
        q = q * scale
        q_l = q.reshape(b, h, m, l, dh).mean(axis=3)
        k_l = k.reshape(b, h, m, l, dh).mean(axis=3)
        sim1 = jnp.einsum('bhid,bhjd->bhij', q, k_l)
        sim2 = jnp.einsum('bhid,bhjd->bhij', q_l, k_l)
        sim3 = jnp.einsum('bhid,bhjd->bhij', q_l, k)
        attn1 = jax.nn.softmax(sim1, axis=-1)
        attn2 = jax.nn.softmax(sim2, axis=-1)
        attn3 = jax.nn.softmax(sim3, axis=-1)
        attn2_inv = _moore_penrose_pinv(attn2, PINV_ITERS)
        out = attn1 @ (attn2_inv @ (attn3 @ v))
        out = out.transpose(0, 2, 1, 3).reshape(b, n, d)
        out = out @ Wout + bout
        return out

    def _L0_ffn_ref(x, Wqkv, q_scale, k_scale, Wo, ln_g, ln_b, W1, b1, W2, b2):
        import jax, jax.numpy as jnp
        import numpy as np
        DIM = 128
        DEPTH = 6
        HEADS = 16
        DIM_HEAD = 64
        WINDOW = 32
        INNER = HEADS * DIM_HEAD
        DIM_INNER = int(DIM * 4 * 2 / 3)
        QK_SCALE = 8.0

        def shift_tokens(t):
            a, s = jnp.split(t, 2, -1)
            s = jnp.pad(s, ((0, 0), (1, 0), (0, 0)))[:, :-1]
            return jnp.concatenate([a, s], -1)

        def l2norm(t):
            return t / jnp.maximum(jnp.linalg.norm(t, axis=-1, keepdims=True), 1e-12)

        def rotate_half(x):
            x1, x2 = jnp.split(x, 2, -1)
            return jnp.concatenate([-x2, x1], -1)

        def rotary_tables(n):
            half = jnp.arange(0, DIM_HEAD, 2, dtype=jnp.float32)
            inv_freq = 1.0 / 10000.0 ** (half / DIM_HEAD)
            t = jnp.arange(n, dtype=jnp.float32)
            freqs = t[:, None] * inv_freq[None, :]
            freqs = jnp.concatenate([freqs, freqs], -1)
            base_scale = (half + 0.4 * DIM_HEAD) / (1.4 * DIM_HEAD)
            power = (t - n // 2) / (WINDOW // 2)
            scale = base_scale[None, :] ** power[:, None]
            scale = jnp.concatenate([scale, scale], -1)
            return (freqs, scale)

        def local_attention(q, k, v):
            b, h, n, d = q.shape
            w = WINDOW
            nw = n // w
            bq = q.reshape(b, h, nw, w, d)
            bk = k.reshape(b, h, nw, w, d)
            bv = v.reshape(b, h, nw, w, d)

            def look(t):
                p = jnp.pad(t, ((0, 0), (0, 0), (1, 0), (0, 0), (0, 0)))
                return jnp.concatenate([p[:, :, :nw], p[:, :, 1:]], axis=3)
            bk2, bv2 = (look(bk), look(bv))
            seq = jnp.arange(n).reshape(nw, w)
            seq_p = jnp.pad(seq, ((1, 0), (0, 0)), constant_values=-1)
            jt = jnp.concatenate([seq_p[:nw], seq_p[1:]], axis=1)
            it = seq[:, :, None]
            jb = jt[:, None, :]
            mask = (it < jb) | (it > jb + w) | (jb == -1)
            sim = jnp.einsum('bhwie,bhwje->bhwij', bq, bk2) * QK_SCALE
            sim = jnp.where(mask, -jnp.finfo(sim.dtype).max, sim)
            attn = jax.nn.softmax(sim, -1)
            out = jnp.einsum('bhwij,bhwje->bhwie', attn, bv2)
            return out.reshape(b, h, n, d)

        def attn_layer(x, Wqkv, qs, ksc, Wo):
            b, n, _ = x.shape
            qkv = x @ Wqkv
            q, k, v = jnp.split(qkv, 3, -1)
            sh = lambda t: t.reshape(b, n, HEADS, DIM_HEAD).transpose(0, 2, 1, 3)
            q, k, v = (sh(q), sh(k), sh(v))
            q = l2norm(q) * qs
            k = l2norm(k) * ksc
            freqs, scale = rotary_tables(n)
            cos, sin = (jnp.cos(freqs), jnp.sin(freqs))
            q = q * cos * scale + rotate_half(q) * sin * scale
            inv = 1.0 / scale
            k = k * cos * inv + rotate_half(k) * sin * inv
            out = local_attention(q, k, v)
            out = out.transpose(0, 2, 1, 3).reshape(b, n, INNER)
            return out @ Wo

        def ffn_layer(x, g, bln, W1, b1, W2, b2):
            mu = x.mean(-1, keepdims=True)
            var = ((x - mu) ** 2).mean(-1, keepdims=True)
            xn = (x - mu) / jnp.sqrt(var + 1e-05) * g + bln
            hg = xn @ W1 + b1
            a, gate = jnp.split(hg, 2, -1)
            return a * jax.nn.gelu(gate, approximate=False) @ W2 + b2
        for i in range(DEPTH):
            x = attn_layer(shift_tokens(x), Wqkv[i], q_scale[i], k_scale[i], Wo[i]) + x
            x = ffn_layer(shift_tokens(x), ln_g[i], ln_b[i], W1[i], b1[i], W2[i], b2[i]) + x
        return x
    x = L0_attn_hidden_states
    xn = _layernorm(x, axis=-1)
    x = x + _L0_attn_ref(xn, L0_attn_Wqkv, L0_attn_bqkv, L0_attn_Wout, L0_attn_bout) + _L0_ffn_ref(xn, L0_ffn_Wqkv, L0_ffn_q_scale, L0_ffn_k_scale, L0_ffn_Wo, L0_ffn_ln_g, L0_ffn_ln_b, L0_ffn_W1, L0_ffn_b1, L0_ffn_W2, L0_ffn_b2)
    return x

_drawn_inputs = setup_inputs


def setup_inputs(seed=0):
    import zlib

    import numpy as np

    out = dict(_drawn_inputs(seed))
    spreads = {'L0_attn_bqkv': (0.0, 0.648),
     'L0_attn_bout': (0.0, 0.468),
     'L0_ffn_q_scale': (1.0, 0.6),
     'L0_ffn_k_scale': (1.0, 0.6),
     'L0_ffn_ln_g': (1.0, 0.6),
     'L0_ffn_ln_b': (0.0, 0.8),
     'L0_ffn_b1': (0.0, 0.8),
     'L0_ffn_b2': (0.0, 0.1)}
    factors = {'L0_attn_Wqkv': 8.0, 'L0_attn_Wout': 4.857, 'L0_ffn_W1': 3.641, 'L0_ffn_W2': 3.576}
    for name, (base, spread) in spreads.items():
        noise = np.random.default_rng([zlib.crc32(name.encode()), seed]).standard_normal(out[name].shape)
        drawn = base * np.exp(spread * noise) if base else spread * noise
        out[name] = jnp.asarray(drawn.astype(out[name].dtype))
    for name, factor in factors.items():
        out[name] = (out[name] * factor).astype(out[name].dtype)
    return out
```

```python
import math
from collections import namedtuple
from contextlib import ExitStack

import numpy as np
import concourse.bass as bass
from concourse import mybir

P = 128
BATCH, SEQ, D = 2, 2048, 128
TOK = BATCH * SEQ
TILES = TOK // P
BT = SEQ // P
DEPTH, HEADS, DH = 6, 16, 64
INNER = HEADS * DH
WIN = 32
WINS = P // WIN
HALF = DH // 2
QK_SCALE = 8.0
FF = int(D * 4 * 2 / 3)
FK = 3
FROWS = [P, P, FF - 2 * P]
XCOLS = SEQ + 1
NH, NDH, NM = 16, 8, 64
NL = SEQ // NM
PINV_ITERS = 6
PAIRS = NH // 2
EPS = 1e-5

UH = HEADS // 2
UW = UH * DH
UP = UH // 2
UNITS = 2 * TILES
ATT_LAG = 4
CHUNK = 4 * P
CHUNKS = TOK // CHUNK
FFN_LAG = 2
LEAD = 4
FLEAD = 2 * FK
QLEAD = 4 * LEAD
R_SCALE = 256.0
MASKED = -1e30
V2_TILE = 16 * 2 * (WINS + 1)
V2_LEAD = 16

C_ROT = 0
C_MASK = C_ROT + 4 * BT * DH
C_IDENT = C_MASK + 2 * UW
C_HALO = C_IDENT + P
C_HEAD = C_HALO + 1
C_PAIR = C_HEAD + NH
C_ALL = C_PAIR + 2 * NDH

B_VAL, B_GATE, B_G, B_B, B_B2, B_ALL = 0, FK, 2 * FK, 2 * FK + 1, 2 * FK + 2, 2 * FK + 3

Unit = namedtuple("Unit", "g half slot tile tg")


def constants():
    half = np.arange(0, DH, 2, dtype=np.float32)
    inv_freq = (1.0 / (np.float32(10000.0) ** (half / np.float32(DH)))).astype(np.float32)
    t = np.arange(SEQ, dtype=np.float32)
    ang = (t[:, None] * inv_freq[None, :]).astype(np.float32).astype(np.float64)
    base = (half.astype(np.float64) + 0.4 * DH) / (1.4 * DH)
    power = ((np.arange(SEQ) % P) - P // 2) / (WIN // 2)
    sc = base[None, :] ** power[:, None]
    cos, sin, sc = (np.concatenate([a, a], -1) for a in (np.cos(ang), np.sin(ang), sc))
    sin[:, :HALF] *= -1.0
    c = np.zeros((P, C_ALL), np.float32)
    for k, tab in enumerate([cos * sc * QK_SCALE, sin * sc * QK_SCALE, cos / sc, sin / sc]):
        a = (tab * R_SCALE).reshape(BT, P, DH).transpose(1, 0, 2).reshape(P, BT * DH)
        c[:, C_ROT + k * BT * DH:C_ROT + (k + 1) * BT * DH] = a
    q = np.arange(P)[:, None] % WIN
    k = np.arange(2 * WIN)[None, :]
    outside = (k < q) | (k > q + WIN)
    first = outside | ((np.arange(P)[:, None] < WIN) & (k < WIN))
    for n, m in enumerate((first, outside)):
        c[:, C_MASK + n * UW:C_MASK + (n + 1) * UW] = np.tile(np.where(m, MASKED, 0.0), (1, UH))
    c[:, C_IDENT:C_IDENT + P] = np.eye(P)
    c[:, C_HALO] = np.tile(base, 4) ** (P / (WIN // 2))
    c[:, C_HEAD:C_HEAD + NH] = np.arange(P)[:, None] // NDH == np.arange(NH)[None, :]
    c[:, C_PAIR:C_ALL] = np.arange(P)[:, None] // NM == np.arange(2 * NDH)[None, :] // NDH
    return c


def upto(n):
    return n + 1 + LEAD


def col(tile):
    return tile * P + tile // BT + 1


def run_steps(eng, layer, step, n_units, lag, unroll, per_tile):
    first = eng.snap(layer * n_units)
    first_tile = eng.snap(layer * (n_units // per_tile))

    def static(s):
        def at(k):
            u = s - k
            if not 0 <= u < n_units:
                return None
            t = u // per_tile
            return Unit(first + u, u % per_tile, t % 2, t, first_tile + t)
        return at

    for s in range(lag):
        step(static(s))
    with eng.Fori(0, (n_units - lag) // unroll) as i:
        now = eng.snap(first + unroll * i)
        tile = eng.snap((unroll // per_tile) * i)
        now_tile = eng.snap(first_tile + (unroll // per_tile) * i)
        for e in range(unroll):
            def at(k, e=e):
                u = lag + e - k
                t = u // per_tile
                return Unit(now + u, u % per_tile, t % 2, tile + t, now_tile + t)
            step(at)
    for s in range(n_units, n_units + lag):
        step(static(s))


def program(nc, hid, a_wqkv, a_bqkv, a_wout, a_bout, wqkv, q_scale, k_scale, wo, ln_g, ln_b, w1, b1, w2, b2,
            const, out):
    fp32, bf16 = mybir.dt.float32, mybir.dt.bfloat16
    ALU, ACT, AX = mybir.AluOpType, mybir.ActivationFunctionType, mybir.AxisListType
    ds = bass.ds

    ctx = ExitStack()
    with ctx:
        def sb(name, shape, dt=fp32, scope=ctx):
            return scope.enter_context(nc.sbuf_tensor(name, shape, dt))

        def sem(name):
            return ctx.enter_context(nc.semaphore(name))

        counted = []

        def csem(name):
            counted.append(sem(name))
            return counted[-1]

        psum = ctx.enter_context(nc.psum_tensor("psum", [P, 8 * 512], fp32))
        bank = [psum[:, i * 512:(i + 1) * 512] for i in range(8)]

        xa = sb("xa", [P, BATCH * XCOLS])
        xb = sb("xb", [P, BATCH * XCOLS])
        consts = sb("consts", [P, C_ALL])
        rot = consts[:, C_ROT:C_MASK].rearrange("p (k t d) -> p k t d", k=4, t=BT)
        ident = consts[:, C_IDENT:C_IDENT + P]
        halo_decay = consts[:, C_HALO:C_HALO + 1]
        identb = sb("identb", [P, P], bf16)
        mask = sb("mask", [P, 2 * UW], bf16)

        a_k_mm, a_kT, a_v_mm, a_vT, a_vtr, a_v = (csem(n) for n in ("a_k_mm", "a_kT", "a_v_mm", "a_vT", "a_vtr", "a_v"))
        b_q, b_s, b_max, b_e, b_rs, b_z = (csem(n) for n in ("b_q", "b_s", "b_max", "b_e", "b_rs", "b_z"))
        b_tr, b_u = sem("b_tr"), sem("b_u")
        b_pT = [sem("b_pT_act"), sem("b_pT_dve")]
        (d_q, d_qT, d_s, d_max, d_sub, d_e, d_sum, d_rd, d_n, d_tr, d_pT, d_o, d_oT, d_y, d_add) = (csem(n) for n in (
            "d_q", "d_qT", "d_s", "d_max", "d_sub", "d_e", "d_sum", "d_rd", "d_n", "d_tr", "d_pT", "d_o", "d_oT", "d_y", "d_add"))

        xs_begun = sem("xs_begun")
        xs_ready = csem("xs_ready")
        q_mm, k_mm, v_mm = csem("q_mm"), csem("k_mm"), csem("v_mm")
        q_raw, q_sq, k_raw, k_sq = (csem(n) for n in ("q_raw", "q_sq", "k_raw", "k_sq"))
        v_raw = csem("v_raw")
        ss_sum, ss_ready = csem("ss_sum"), csem("ss_ready")
        ln_done, r0_ready = csem("ln_done"), csem("r0_ready")
        nt_sq, nt_half, r_ready = csem("nt_sq"), csem("nt_half"), csem("r_ready")
        qn_ready, kn_ready = csem("qn_ready"), csem("kn_ready")
        cos_done, sin_done, rot_ready = csem("cos_done"), csem("sin_done"), csem("rot_ready")
        qT_mm, kT_mm = csem("qT_mm"), csem("kT_mm")
        qT_ready, halo_ready, kb_ready = csem("qT_ready"), csem("halo_ready"), csem("kb_ready")
        s_mm, max_done, sub_done, e_ready = (csem(n) for n in ("s_mm", "max_done", "sub_done", "e_ready"))
        den_done, rden_ready = csem("den_done"), csem("rden_ready")
        pT_mm, pT_ready, av_mm, o_ready = (csem(n) for n in ("pT_mm", "pT_ready", "av_mm", "o_ready"))
        oT_mm, oT_ready, y_mm = csem("oT_mm"), csem("oT_ready"), csem("y_mm")
        y_used = csem("y_used")
        v2_ready = [sem("v2_ready0"), sem("v2_ready1")]
        f1_low = csem("f1_low")
        f1_x, f1_mm, f1_tok, f1_stat = (csem(n) for n in ("f1_x", "f1_mm", "f1_tok", "f1_stat"))
        f_stat = sem("f_stat")
        f_ln = sem("f_ln")
        f2_norm, f2_tr, f2_xT = csem("f2_norm"), csem("f2_tr"), csem("f2_xT")
        f2_gate, f2_val, f2_gelu, f2_h = (sem(n) for n in ("f2_gate", "f2_val", "f2_gelu", "f2_h"))
        f2_y, f2_res = csem("f2_y"), csem("f2_res")
        f_par, f_tab, w_att, w_ffn = sem("f_par"), sem("f_tab"), sem("w_att"), sem("w_ffn")
        fin_in, fin_x, fin_mm, fin_add, fin_out = (sem(n) for n in ("fin_in", "fin_x", "fin_mm", "fin_add", "fin_out"))
        loaded, s_init, s_stat, s_ln, s_norm, s_tr, s_put = (
            sem(n) for n in ("loaded", "s_init", "s_stat", "s_ln", "s_norm", "s_tr", "s_put"))

        def finish_stats(dve, stats, small, count, base):
            mean, var, diff = small[:, 0, :], small[:, 1, :], small[:, 2, :]
            nc.vector.tensor_tensor(mean, stats[:, :, 1], stats[:, :, 4], ALU.add).then_inc(count, 1)
            nc.vector.tensor_tensor(diff, stats[:, :, 1], stats[:, :, 4], ALU.subtract).then_inc(count, 1)
            nc.vector.tensor_tensor(var, stats[:, :, 2], stats[:, :, 5], ALU.add).then_inc(count, 1)
            dve.wait_ge(count, base + 3)
            nc.vector.tensor_scalar(mean, mean, 0.5, None, ALU.mult).then_inc(count, 1)
            nc.vector.tensor_tensor(diff, diff, diff, ALU.mult).then_inc(count, 1)
            nc.vector.tensor_scalar(var, var, 1.0 / D, EPS, ALU.mult, ALU.add).then_inc(count, 1)
            dve.wait_ge(count, base + 6)
            nc.vector.scalar_tensor_tensor(out=var, in0=diff, scalar=0.25, in1=var, op0=ALU.mult,
                                           op1=ALU.add).then_inc(count, 1)

        def rsqrt_seed(act, small, count, base):
            nc.scalar.activation(small[:, 3, :], small[:, 1, :], ACT.Ln).then_inc(count, 1)
            act.wait_ge(count, base + 1)
            nc.scalar.activation(small[:, 4, :], small[:, 3, :], ACT.Exp, scale=-0.5).then_inc(count, 1)

        def rsqrt_refine(dve, small, count, base):
            var, sq, r = small[:, 1, :], small[:, 5, :], small[:, 4, :]
            nc.vector.tensor_tensor(sq, r, r, ALU.mult).then_inc(count, 1)
            dve.wait_ge(count, base + 1)
            nc.vector.scalar_tensor_tensor(out=sq, in0=sq, scalar=-0.5, in1=var, op0=ALU.mult,
                                           op1=ALU.mult).then_inc(count, 1)
            dve.wait_ge(count, base + 2)
            nc.vector.scalar_tensor_tensor(out=r, in0=sq, scalar=1.5, in1=r, op0=ALU.add,
                                           op1=ALU.mult).then_inc(count, 1)
        STATS, REFINE = 7, 3

        with ExitStack() as scope:
            xtok = sb("xtok", [P, TILES, D], scope=scope)
            stats = sb("stats0", [P, TILES, 6], scope=scope)
            small = sb("small0", [P, 6, TILES], scope=scope)
            xn = sb("xn0", [P, 2, P], scope=scope)
            with nc.Block() as block:
                @block.sync
                def _(sp):
                    sp.dma_start(xtok[:, :, :], hid.rearrange("b (n p) d -> p (b n) d", p=P)).then_inc(loaded, 16)
                    sp.dma_start(consts[:, :], const).then_inc(loaded, 16)
                    sp.wait_ge(loaded, 32)

                @block.gpsimd
                def _(pool):
                    for x in (xa, xb):
                        for b in range(BATCH):
                            nc.gpsimd.memset(x[:, b * XCOLS:b * XCOLS + 1], 0.0).then_inc(s_init, 1)
                    for s in counted:
                        pool.sem_inc(s, LEAD)
                    for s in (f2_gate, f2_val, f2_gelu, f2_h):
                        pool.sem_inc(s, FLEAD)
                    for s in (b_tr, b_u):
                        pool.sem_inc(s, QLEAD)
                    for s in b_pT:
                        pool.sem_inc(s, QLEAD // 2)
                    for s in v2_ready:
                        pool.sem_inc(s, V2_LEAD)
                    for s in (s_tr, s_put, fin_mm, fin_add):
                        pool.sem_inc(s, 1)

                @block.vector
                def _(dve):
                    dve.wait_ge(loaded, 32)
                    nc.vector.tensor_copy(identb[:, :], ident).then_inc(s_init, 1)
                    nc.vector.tensor_copy(mask[:, :], consts[:, C_MASK:C_IDENT]).then_inc(s_init, 1)
                    with dve.Fori(0, TILES) as t:
                        nc.vector.bn_stats(stats[:, ds(t, 1), :].rearrange("p a b -> p (a b)"),
                                           xtok[:, ds(t, 1), :].rearrange("p a b -> p (a b)")).then_inc(s_stat, 1)
                    dve.wait_ge(s_stat, TILES)
                    finish_stats(dve, stats, small, s_stat, TILES)
                    dve.wait_ge(s_ln, 2)
                    rsqrt_refine(dve, small, s_norm, 0)
                    dve.wait_ge(s_norm, REFINE)
                    with dve.Fori(0, TILES // 2) as i:
                        for e in range(2):
                            t = 2 * i + e
                            dve.wait_ge(s_tr, t + 1)
                            nc.vector.tensor_scalar(xn[:, e, :], xtok[:, ds(t, 1), :].rearrange("p a b -> p (a b)"),
                                                    small[:, 0, ds(t, 1)], small[:, 4, ds(t, 1)], ALU.subtract,
                                                    ALU.mult).then_inc(s_norm, 1)

                @block.scalar
                def _(act):
                    nc.scalar.preload_act_table_set("natural_log_exp_and_others")
                    act.wait_ge(s_stat, TILES + STATS)
                    rsqrt_seed(act, small, s_ln, 0)
                    with act.Fori(0, TILES // 2) as i:
                        for e in range(2):
                            t = 2 * i + e
                            act.wait_ge(s_tr, t + 2)
                            nc.scalar.copy(xa[:, ds(col(t), P)], bank[e][:, 0:P]).then_inc(s_put, 1)

                @block.tensor
                def _(pe):
                    pe.wait_ge(loaded, 32)
                    with pe.Fori(0, TILES // 2) as i:
                        for e in range(2):
                            t = 2 * i + e
                            pe.wait_ge(s_norm, REFINE + t + 1)
                            pe.wait_ge(s_put, t + 1)
                            nc.tensor.transpose(bank[e][:, 0:P], xn[:, e, :], ident).then_inc(s_tr, 1)

        att_out = nc.dram_tensor("att_out", [TOK, D], fp32).ap()
        with ExitStack() as scope:
            aw = sb("aw", [P, 3 * D], scope=scope)
            awout = sb("awout", [P, D], scope=scope)
            ab = sb("ab", [P, 3], scope=scope)
            about = sb("about", [P, D], scope=scope)
            xh = sb("xh", [P, TILES, D], scope=scope)
            kT = sb("kT_a", [P, TOK], scope=scope)
            vt = sb("vt_a", [P, TILES, D], scope=scope)
            vTc = sb("vTc", [P, 2, CHUNK], scope=scope)
            xl = sb("xl", [P, BATCH, NM], scope=scope)
            ql, kl = sb("ql", [P, BATCH, NM], scope=scope), sb("kl", [P, BATCH, NM], scope=scope)
            qlb = sb("qlb", [P, BATCH, NH, NM], scope=scope)
            klb = sb("klb", [P, BATCH, NH, NM], scope=scope)
            zb = sb("zb", [P, BATCH * PAIRS, 2 * NDH], scope=scope)
            yb = sb("yb", [P, BATCH * PAIRS, 2 * NDH], scope=scope)
            qscale = 1.0 / math.sqrt(NDH)
            a_in, a_bias, a_land, a_lp, a_ql = (sem(n) for n in ("a_in", "a_bias", "a_land", "a_lp", "a_ql"))

            with nc.Block() as block:
                @block.sync
                def _(sp):
                    sp.dma_start(aw[:, :], a_wqkv).then_inc(a_in, 16)
                    with nc.allow_non_contiguous_dma(reason="a few per-feature parameters"):
                        sp.dma_start(ab[:, :], a_bqkv.rearrange("(k p) -> p k", p=P)).then_inc(a_in, 16)
                    sp.dma_start(awout[:, :], a_wout).then_inc(a_in, 16)
                    sp.dma_start(about[:, :], a_bout.partition_broadcast(P)).then_inc(a_in, 16)
                    sp.dma_start(xh[:, :, :], hid.rearrange("b (n p) d -> p (b n) d", p=P)).then_inc(a_in, 16)
                    sp.wait_ge(a_in, 80)

                @block.gpsimd
                def _(pool):
                    pool.wait_ge(a_in, 80)
                    nc.gpsimd.tensor_tensor(xh[:, :, :], xh[:, :, :], about[:, :].unsqueeze(1).broadcast_to([P, TILES, D]),
                                            ALU.add).then_inc(a_bias, 1)

                @block.vector
                def _(dve):
                    for b in range(BATCH):
                        nc.vector.tensor_reduce(xl[:, b, :], xa[:, b * XCOLS + 1:(b + 1) * XCOLS].rearrange("p (m l) -> p m l", l=NL),
                                                AX.X, ALU.add).then_inc(a_land, 1)
                    dve.wait_ge(a_in, 80)
                    nc.vector.tensor_scalar(ab[:, 0:1], ab[:, 0:1], qscale, None, ALU.mult).then_inc(a_bias, 1)
                    dve.wait_ge(a_bias, 2)
                    dve.wait_ge(a_lp, 2)
                    nc.vector.tensor_scalar(ql[:, :, :], bank[0][:, 0:BATCH * NM].rearrange("p (b m) -> p b m", b=BATCH), qscale / NL, ab[:, 0:1],
                                            ALU.mult, ALU.add).then_inc(a_ql, 1)
                    nc.vector.tensor_scalar(kl[:, :, :], bank[1][:, 0:BATCH * NM].rearrange("p (b m) -> p b m", b=BATCH), 1.0 / NL, ab[:, 1:2],
                                            ALU.mult, ALU.add).then_inc(a_ql, 1)
                    dve.wait_ge(a_ql, 2)
                    heads = consts[:, C_HEAD:C_HEAD + NH].unsqueeze(2).broadcast_to([P, NH, NM])
                    for b in range(BATCH):
                        for src, dst in ((ql, qlb), (kl, klb)):
                            nc.vector.tensor_tensor(dst[:, b, :, :], src[:, b, :].unsqueeze(1).broadcast_to([P, NH, NM]),
                                                    heads, ALU.mult).then_inc(a_ql, 1)

                @block.scalar
                def _(act):
                    def step(at):
                        u = at(0)
                        if u:
                            act.wait_ge(a_k_mm, upto(u.g))
                            nc.scalar.activation(kT[:, ds(u.tile * CHUNK, CHUNK)], bank[2 + u.slot][:, :], ACT.Identity,
                                                 bias=ab[:, 1:2]).then_inc(a_kT, 1)
                            act.wait_ge(a_v_mm, upto(u.g))
                            act.wait_ge(a_vtr, upto(u.g - 2))
                            nc.scalar.activation(vTc[:, u.slot, :], bank[4 + u.slot][:, :], ACT.Identity,
                                                 bias=ab[:, 2:3]).then_inc(a_vT, 1)
                        u = at(1)
                        if u:
                            act.wait_ge(a_vtr, upto(u.g))
                            nc.scalar.copy(vt[:, ds(u.tile * 4, 4), :], bank[6 + u.slot][:, :].rearrange("p (a c) -> p a c", a=4))\
                                .then_inc(a_v, 1)
                    run_steps(act, 0, step, CHUNKS, 2, 2, 1)

                @block.tensor
                def _(pe):
                    pe.wait_ge(a_in, 80)
                    pe.wait_ge(a_land, 2)
                    for k in range(2):
                        nc.tensor.matmul(bank[k][:, 0:BATCH * NM], aw[:, k * D:(k + 1) * D], xl[:, :, :].rearrange("p b m -> p (b m)"),
                                         start=True, stop=True).then_inc(a_lp, 1)

                    def step(at):
                        u = at(0)
                        if u:
                            x = xa[:, ds(u.tile * CHUNK + u.tile // (CHUNKS // BATCH) + 1, CHUNK)]
                            pe.wait_ge(a_kT, upto(u.g - 2))
                            nc.tensor.matmul(bank[2 + u.slot][:, :], aw[:, D:2 * D], x, start=True, stop=True).then_inc(a_k_mm, 1)
                            pe.wait_ge(a_vT, upto(u.g - 2))
                            nc.tensor.matmul(bank[4 + u.slot][:, :], aw[:, 2 * D:3 * D], x, start=True, stop=True).then_inc(a_v_mm, 1)
                        u = at(1)
                        if u:
                            pe.wait_ge(a_vT, upto(u.g))
                            pe.wait_ge(a_v, upto(u.g - 2))
                            for j in range(4):
                                last = nc.tensor.transpose(bank[6 + u.slot][:, j * P:(j + 1) * P], vTc[:, u.slot, j * P:(j + 1) * P], ident)
                            last.then_inc(a_vtr, 1)
                    run_steps(pe, 0, step, CHUNKS, 2, 2, 1)

            with ExitStack() as inner:
                qb = sb("qb_a", [P, 2, P], scope=inner)
                p3 = sb("p3", [P, 2, SEQ], scope=inner)
                p3T = sb("p3T", [P, 2, CHUNK], scope=inner)
                nmx = sb("nmx", [P, 2], scope=inner)
                sum3, rsum3 = sb("sum3", [P, 2], scope=inner), sb("rsum3", [P, 2], scope=inner)
                s3 = psum[:, 0:SEQ]
                with nc.Block() as block:
                    @block.vector
                    def _(dve):
                        def step(at):
                            u = at(0)
                            if u:
                                dve.wait_ge(b_s, upto(u.g - 2))
                                nc.vector.tensor_copy(qb[:, u.slot, :], qlb[:, :, :, :].rearrange("p b h m -> p (b h m)")[:, ds(u.tile * P, P)])\
                                    .then_inc(b_q, 1)
                            u = at(1)
                            if u:
                                for j in (1, 3):
                                    dve.wait_ge(b_tr, QLEAD + 4 * u.g + j + 1)
                                    dve.wait_ge(b_u, QLEAD + 4 * u.g + j - 1)
                                    nc.vector.tensor_copy(p3T[:, 1, :], bank[5][:, :]).then_inc(b_pT[1], 1)
                                dve.wait_ge(b_rs, upto(u.g))
                                dve.wait_ge(b_u, QLEAD + 4 * u.g + 4)
                                nc.vector.scalar_tensor_tensor(
                                    out=zb[:, ds(u.tile, 1), :].rearrange("p a b -> p (a b)"),
                                    in0=bank[6][:, ds((u.tile % PAIRS) * 2 * NDH, 2 * NDH)],
                                    scalar=rsum3[:, u.slot:u.slot + 1], in1=consts[:, C_PAIR:C_ALL], op0=ALU.mult,
                                    op1=ALU.mult).then_inc(b_z, 1)
                            u = at(0)
                            if u:
                                dve.wait_ge(b_s, upto(u.g))
                                dve.wait_ge(b_e, upto(u.g - 2))
                                nc.vector.tensor_reduce(nmx[:, u.slot:u.slot + 1], s3, AX.X, ALU.max, negate=True).then_inc(b_max, 1)
                                dve.wait_ge(b_e, upto(u.g))
                                dve.wait_ge(b_z, upto(u.g - 2))
                                nc.vector.reciprocal(rsum3[:, u.slot:u.slot + 1], sum3[:, u.slot:u.slot + 1]).then_inc(b_rs, 1)
                        run_steps(dve, 0, step, BATCH * PAIRS, 2, 2, 1)

                    @block.scalar
                    def _(act):
                        nc.scalar.preload_act_table_set("natural_log_exp_and_others")

                        def step(at):
                            u = at(1)
                            if u:
                                for j in (0, 2):
                                    act.wait_ge(b_tr, QLEAD + 4 * u.g + j + 1)
                                    act.wait_ge(b_u, QLEAD + 4 * u.g + j - 1)
                                    nc.scalar.copy(p3T[:, 0, :], bank[4][:, :]).then_inc(b_pT[0], 1)
                            u = at(0)
                            if u:
                                act.wait_ge(b_max, upto(u.g))
                                act.wait_ge(b_tr, QLEAD + 4 * (u.g - 2) + 4)
                                act.wait_ge(b_rs, upto(u.g - 2))
                                nc.scalar.activation(p3[:, u.slot, :], s3, ACT.Exp, bias=nmx[:, u.slot:u.slot + 1],
                                                     accum_out=sum3[:, u.slot:u.slot + 1]).then_inc(b_e, 1)
                        run_steps(act, 0, step, BATCH * PAIRS, 2, 2, 1)

                    @block.tensor
                    def _(pe):
                        def step(at):
                            u = at(0)
                            if u:
                                pe.wait_ge(b_q, upto(u.g))
                                pe.wait_ge(b_e, upto(u.g - 1))
                                for c in range(SEQ // CHUNK):
                                    last = nc.tensor.matmul(bank[c][:, :], qb[:, u.slot, :],
                                                            kT[:, ds((u.tile // PAIRS) * SEQ + c * CHUNK, CHUNK)], start=True, stop=True)
                                last.then_inc(b_s, 1)
                            u = at(1)
                            if u:
                                pe.wait_ge(b_e, upto(u.g))
                                pe.wait_ge(b_z, upto(u.g - 1))
                                for j in range(5):
                                    if j < 4:
                                        pe.wait_ge(b_pT[j % 2], QLEAD // 2 + 2 * u.g + j // 2)
                                        for i in range(4):
                                            last = nc.tensor.transpose(bank[4 + j % 2][:, i * P:(i + 1) * P],
                                                                       p3[:, u.slot, (4 * j + i) * P:(4 * j + i + 1) * P], ident)
                                        last.then_inc(b_tr, 1)
                                    if j > 0:
                                        pe.wait_ge(b_pT[(j - 1) % 2], QLEAD // 2 + 2 * u.g + (j - 1) // 2 + 1)
                                        for i in range(4):
                                            n = 4 * (j - 1) + i
                                            last = nc.tensor.matmul(
                                                bank[6][:, 0:D], p3T[:, (j - 1) % 2, i * P:(i + 1) * P],
                                                vt[:, ds((u.tile // PAIRS) * BT + n, 1), :].rearrange("p a b -> p (a b)"),
                                                start=(n == 0), stop=(n == BT - 1))
                                        last.then_inc(b_u, 1)
                        run_steps(pe, 0, step, BATCH * PAIRS, 2, 2, 1)

            with ExitStack() as inner:
                GR = 4
                mats = {n: sb(n, [P, GR, GR, P], scope=inner) for n in ("x2", "x2T", "vi", "viT", "kvT", "ti")}
                x2, x2T, vi, viT, kvT, ti = mats.values()
                e2 = sb("e2", [P, BATCH * PAIRS, NM], scope=inner)
                m2, d2 = sb("m2", [P, BATCH * PAIRS], scope=inner), sb("d2", [P, BATCH * PAIRS], scope=inner)
                idc = sb("idc", [P, 3, P], scope=inner)
                c_s, c_x, c_xT = sem("c_s"), sem("c_x"), sem("c_xT")
                i_v, i_kv, i_kvT, i_t1, i_a, i_t2, i_b, i_t3, i_vn = (
                    sem(n) for n in ("i_v", "i_kv", "i_kvT", "i_t1", "i_a", "i_t2", "i_b", "i_t3", "i_vn"))
                y_mm_a, y_rd = sem("y_mm_a"), sem("y_rd")
                with nc.Block() as block:
                    @block.tensor
                    def _(pe):
                        for n in range(BATCH * PAIRS):
                            b, c = n // PAIRS, n % PAIRS
                            last = nc.tensor.matmul(bank[b][:, c * NM:(c + 1) * NM], qlb[:, b, 2 * c:2 * c + 2, :].rearrange("p h m -> p (h m)"),
                                                    kl[:, b, :], start=True, stop=True)
                        last.then_inc(c_s, 1)
                        pe.wait_ge(c_x, 9)
                        for g in range(GR):
                            for j in range(GR):
                                last = nc.tensor.transpose(bank[2 + g][:, j * P:(j + 1) * P], x2[:, g, j, :], ident)
                            last.then_inc(c_xT, 1)

                    @block.gpsimd
                    def _(pool):
                        nc.gpsimd.memset(x2[:, :, :, :], 0.0)
                        for k, v in enumerate((7.0, 15.0, 13.0)):
                            last = nc.gpsimd.tensor_scalar(idc[:, k, :], ident, v, None, ALU.mult)
                        last.then_inc(c_x, 1)
                        pool.sem_inc(i_vn, GR)

                    @block.vector
                    def _(dve):
                        s2 = psum[:, 0:BATCH * PAIRS * NM].rearrange("p (n m) -> p n m", m=NM)
                        dve.wait_ge(c_s, 1)
                        nc.vector.tensor_reduce(m2[:, :], s2, AX.X, ALU.max).then_inc(c_x, 1)
                        dve.wait_ge(c_x, 2)
                        nc.vector.tensor_tensor(e2[:, :, :], s2, m2[:, :].unsqueeze(2).broadcast_to([P, BATCH * PAIRS, NM]),
                                                ALU.subtract).then_inc(c_x, 1)
                        dve.wait_ge(c_x, 4)
                        nc.vector.tensor_reduce(d2[:, :], e2[:, :, :], AX.X, ALU.add).then_inc(c_x, 1)
                        dve.wait_ge(c_x, 5)
                        nc.vector.reciprocal(m2[:, :], d2[:, :]).then_inc(c_x, 1)
                        dve.wait_ge(c_x, 6)
                        x2f = x2[:, :, :, :].rearrange("p g j c -> p (g j) c")
                        for h in range(2):
                            rows = slice(64 * h, 64 * h + 64)
                            nc.vector.tensor_tensor(x2f[rows, :, 64 * h:64 * h + 64], e2[rows, :, :],
                                                    m2[rows, :].unsqueeze(2).broadcast_to([64, BATCH * PAIRS, NM]),
                                                    ALU.mult).then_inc(c_x, 1)
                        dve.wait_ge(c_x, 8)
                        nc.vector.tensor_copy(vi[:, :, :, :], x2[:, :, :, :]).then_inc(c_x, 1)

                    @block.scalar
                    def _(act):
                        act.wait_ge(c_x, 3)
                        nc.scalar.activation(e2[:, :, :], e2[:, :, :], ACT.Exp).then_inc(c_x, 1)
                        for g in range(GR):
                            act.wait_ge(c_xT, g + 1)
                            src = bank[2 + g][:, :].rearrange("p (j c) -> p j c", j=GR)
                            nc.scalar.copy(x2T[:, g, :, :], src)
                            nc.scalar.copy(viT[:, g, :, :], src).then_inc(i_v, 1)

                with nc.Block() as block:
                    def product(out_bank, left_T, right, g, count):
                        for j in range(GR):
                            last = nc.tensor.matmul(out_bank[:, j * P:(j + 1) * P], left_T[:, g, j, :], right[:, g, j, :],
                                                    start=True, stop=True)
                        if count is not None:
                            last.then_inc(count, 1)

                    @block.tensor
                    def _(pe):
                        with pe.Fori(0, PINV_ITERS) as it:
                            n = pe.snap(GR * it)
                            for g in range(GR):
                                pe.wait_ge(i_v, n + g + 1)
                                product(bank[2 * g], x2T, vi, g, None)
                                product(bank[2 * g + 1], vi, x2T, g, i_kv)
                            for g in range(GR):
                                pe.wait_ge(i_kvT, n + g + 1)
                                pe.wait_ge(i_t1, n + g + 1)
                                product(bank[2 * g], kvT, ti, g, i_a)
                            for g in range(GR):
                                pe.wait_ge(i_t2, n + g + 1)
                                product(bank[2 * g], kvT, ti, g, i_b)
                            for g in range(GR):
                                pe.wait_ge(i_t3, n + g + 1)
                                product(bank[2 * g], viT, ti, g, None)
                                product(bank[2 * g + 1], ti, viT, g, i_vn)
                        pe.wait_ge(i_v, GR * PINV_ITERS + GR)
                        for m in range(BATCH * PAIRS):
                            last = nc.tensor.matmul(bank[0][:, m * 2 * NDH:(m + 1) * 2 * NDH], viT[:, m // GR, m % GR, :],
                                                    zb[:, m, :], start=True, stop=True)
                        last.then_inc(y_mm_a, 1)

                    @block.vector
                    def _(dve):
                        with dve.Fori(0, PINV_ITERS) as it:
                            n = dve.snap(GR * it)
                            for k, (ready, done) in enumerate(((i_kv, i_t1), (i_a, i_t2), (i_b, i_t3))):
                                for g in range(GR):
                                    dve.wait_ge(ready, n + g + 1)
                                    if k == 0:
                                        dve.wait_ge(i_vn, n + g + 1)
                                    nc.vector.tensor_tensor(ti[:, g, :, :], idc[:, k, :].unsqueeze(1).broadcast_to([P, GR, P]),
                                                            bank[2 * g][:, :].rearrange("p (j c) -> p j c", j=GR),
                                                            ALU.subtract).then_inc(done, 1)
                        dve.wait_ge(y_mm_a, 1)
                        nc.vector.tensor_copy(yb[:, :, :], bank[0][:, 0:BATCH * PAIRS * 2 * NDH].rearrange("p (n c) -> p n c", c=2 * NDH))\
                            .then_inc(y_rd, 1)

                    @block.scalar
                    def _(act):
                        with act.Fori(0, PINV_ITERS) as it:
                            n = act.snap(GR * it)
                            for g in range(GR):
                                act.wait_ge(i_kv, n + g + 1)
                                nc.scalar.copy(kvT[:, g, :, :], bank[2 * g + 1][:, :].rearrange("p (j c) -> p j c", j=GR)).then_inc(i_kvT, 1)
                            for g in range(GR):
                                act.wait_ge(i_vn, n + GR + g + 1)
                                nc.scalar.mul(vi[:, g, :, :], bank[2 * g][:, :].rearrange("p (j c) -> p j c", j=GR), 0.25)
                                nc.scalar.mul(viT[:, g, :, :], bank[2 * g + 1][:, :].rearrange("p (j c) -> p j c", j=GR), 0.25).then_inc(i_v, 1)

            with ExitStack() as inner:
                yp = sb("yp", [P, PAIRS * (P + 2 * NDH)], scope=inner)
                qTa = sb("qTa", [P, 2, P], scope=inner)
                sub1 = sb("sub1", [P, NH, NM], scope=inner)
                m1, d1, rd1 = sb("m1", [P, NH], scope=inner), sb("d1", [P, NH], scope=inner), sb("rd1", [P, 2, NH], scope=inner)
                p1 = sb("p1", [P, 2, NH, NM], scope=inner)
                p1T = sb("p1T", [P, 2, PAIRS, P], scope=inner)
                oTa = sb("oTa", [P, 2, P], scope=inner)
                s1 = psum[:, 512:512 + NH * NM].rearrange("p (h m) -> p h m", m=NM)
                d_yp = sem("d_yp")
                a_store = sem("a_store")
                with nc.Block() as block:
                    @block.gpsimd
                    def _(pool):
                        nc.gpsimd.memset(yp[:, :], 0.0).then_inc(d_yp, 1)

                with nc.Fori(0, BATCH) as b:
                    with nc.Block() as block:
                        @block.gpsimd
                        def _(pool):
                            nc.gpsimd.tensor_copy(yp[:, :].rearrange("p (n c) -> p n c", n=PAIRS)[:, :, 0:2 * NDH],
                                                  yb[:, ds(b * PAIRS, PAIRS), :]).then_inc(d_yp, 1)

                            def step(at):
                                u = at(0)
                                if u:
                                    pool.wait_ge(d_rd, upto(u.g))
                                    nc.gpsimd.tensor_tensor(p1[:, u.slot, :, :], p1[:, u.slot, :, :],
                                                            rd1[:, u.slot, :].unsqueeze(2).broadcast_to([P, NH, NM]), ALU.mult).then_inc(d_n, 1)
                            run_steps(pool, b, step, BT, 2, 2, 1)

                        @block.scalar
                        def _(act):
                            def step(at):
                                u = at(0)
                                if u:
                                    act.wait_ge(d_q, upto(u.g))
                                    act.wait_ge(d_s, upto(u.g - 2))
                                    nc.scalar.activation(qTa[:, u.slot, :], bank[0][:, 0:P], ACT.Identity, scale=qscale, bias=ab[:, 0:1])\
                                        .then_inc(d_qT, 1)
                                u = at(1)
                                if u:
                                    act.wait_ge(d_tr, upto(u.g))
                                    act.wait_ge(d_o, upto(u.g - 2))
                                    nc.scalar.copy(p1T[:, u.slot, :, :], psum[:, 3 * 512:5 * 512].rearrange("p (n c) -> p n c", n=PAIRS)).then_inc(d_pT, 1)
                                u = at(0)
                                if u:
                                    act.wait_ge(d_sub, upto(u.g))
                                    act.wait_ge(d_tr, upto(u.g - 2))
                                    nc.scalar.activation(p1[:, u.slot, :, :], sub1[:, :, :], ACT.Exp).then_inc(d_e, 1)
                                u = at(1)
                                if u:
                                    act.wait_ge(d_o, upto(u.g))
                                    act.wait_ge(d_y, upto(u.g - 2))
                                    nc.scalar.copy(oTa[:, u.slot, :], bank[5][:, 0:P]).then_inc(d_oT, 1)
                            run_steps(act, b, step, BT, 2, 2, 1)

                        @block.vector
                        def _(dve):
                            def step(at):
                                u = at(0)
                                if u:
                                    dve.wait_ge(d_s, upto(u.g))
                                    dve.wait_ge(d_sub, upto(u.g - 1))
                                    nc.vector.tensor_reduce(m1[:, :], s1, AX.X, ALU.max).then_inc(d_max, 1)
                                    dve.wait_ge(d_max, upto(u.g))
                                    dve.wait_ge(d_e, upto(u.g - 1))
                                    nc.vector.tensor_tensor(sub1[:, :, :], s1, m1[:, :].unsqueeze(2).broadcast_to([P, NH, NM]), ALU.subtract)\
                                        .then_inc(d_sub, 1)
                                u = at(2)
                                if u:
                                    dve.wait_ge(d_y, upto(u.g))
                                    a = xh[:, ds(b * BT + u.tile, 1), :].rearrange("p a b -> p (a b)")
                                    nc.vector.tensor_tensor(a, bank[6][:, 0:D], a, ALU.add).then_inc(d_add, 1)
                                u = at(0)
                                if u:
                                    dve.wait_ge(d_e, upto(u.g))
                                    dve.wait_ge(d_rd, upto(u.g - 1))
                                    nc.vector.tensor_reduce(d1[:, :], p1[:, u.slot, :, :], AX.X, ALU.add).then_inc(d_sum, 1)
                                    dve.wait_ge(d_sum, upto(u.g))
                                    dve.wait_ge(d_n, upto(u.g - 2))
                                    nc.vector.reciprocal(rd1[:, u.slot, :], d1[:, :]).then_inc(d_rd, 1)
                            run_steps(dve, b, step, BT, 2, 2, 1)

                        @block.tensor
                        def _(pe):
                            pe.wait_ge(d_yp, b + 2)

                            def step(at):
                                u = at(0)
                                if u:
                                    pe.wait_ge(d_qT, upto(u.g - 1))
                                    nc.tensor.matmul(bank[0][:, 0:P], aw[:, 0:D], xa[:, ds(b * XCOLS + 1 + u.tile * P, P)], start=True, stop=True)\
                                        .then_inc(d_q, 1)
                                u = at(1)
                                if u:
                                    pe.wait_ge(d_n, upto(u.g))
                                    pe.wait_ge(d_pT, upto(u.g - 1))
                                    for c in range(PAIRS):
                                        last = nc.tensor.transpose(psum[:, 3 * 512 + c * P:3 * 512 + (c + 1) * P],
                                                                   p1[:, u.slot, 2 * c:2 * c + 2, :].rearrange("p h m -> p (h m)"), ident)
                                    last.then_inc(d_tr, 1)
                                u = at(0)
                                if u:
                                    pe.wait_ge(d_qT, upto(u.g))
                                    pe.wait_ge(d_sub, upto(u.g - 1))
                                    for c in range(2):
                                        last = nc.tensor.matmul(bank[1 + c][:, :], qTa[:, u.slot, :],
                                                                klb[:, ds(b, 1), c * 8:(c + 1) * 8, :].rearrange("p b h m -> p (b h m)"),
                                                                start=True, stop=True)
                                    last.then_inc(d_s, 1)
                                u = at(2)
                                if u:
                                    pe.wait_ge(d_oT, upto(u.g))
                                    pe.wait_ge(d_add, upto(u.g - 1))
                                    nc.tensor.matmul(bank[6][:, 0:D], oTa[:, u.slot, :], awout[:, :], start=True, stop=True).then_inc(d_y, 1)
                                u = at(1)
                                if u:
                                    pe.wait_ge(d_pT, upto(u.g))
                                    pe.wait_ge(d_oT, upto(u.g - 1))
                                    for c in range(PAIRS):
                                        last = nc.tensor.matmul(bank[5][:, 0:P], yp[:, c * P:(c + 1) * P], p1T[:, u.slot, c, :],
                                                                start=(c == 0), stop=(c == PAIRS - 1))
                                    last.then_inc(d_o, 1)
                            run_steps(pe, b, step, BT, 2, 2, 1)

                with nc.Block() as block:
                    @block.sync
                    def _(sp):
                        sp.dma_start(att_out.rearrange("(n p) d -> p n d", p=P), xh[:, :, :]).then_inc(a_store, 16)
                        sp.wait_ge(a_store, 16)
        att_src = att_out

        wqkv_sb = sb("wqkv_sb", [P, 3 * INNER])
        wo_sb = sb("wo_sb", [P, HEADS // 2, D])
        w1_sb = sb("w1_sb", [P, 2 * FF])
        w2_sb = sb("w2_sb", [P, FK, D])
        tab = sb("tab", [P, 4, BT, DH])
        scales = sb("scales", [P, 4, DEPTH, DH])
        par_all = sb("par_all", [P, DEPTH, B_ALL])
        par = sb("par", [P, B_ALL])
        vtok = sb("vtok", [P, 2, 2, 2, UP * DH])
        v2 = sb("v2", [P, 2, WINS, 2, 2, UP * DH])
        kb = sb("kb", [P, 2, UP, 2, WIN + P])

        def load_att_weights(sp, layer):
            sp.dma_start(wqkv_sb[:, :], wqkv[ds(layer, 1), :, :].rearrange("l p n -> (l p) n")).then_inc(w_att, 16)
            sp.dma_start(wo_sb[:, :, :], wo[ds(layer, 1), :, :].rearrange("l (c p) n -> (l p) c n", p=P)).then_inc(w_att, 16)

        def make_tables(pool, layer, count):
            for k in range(4):
                nc.gpsimd.tensor_tensor(tab[:, k, :, :], rot[:, k, :, :],
                                        scales[:, k, ds(layer, 1), :].broadcast_to([P, BT, DH]),
                                        ALU.mult).then_inc(count, 1)

        with nc.Block() as block:
            @block.sync
            def _(sp):
                load_att_weights(sp, 0)
                loads = []
                for k, src in ((0, q_scale), (2, k_scale)):
                    loads.append((scales[:, k, :, :], src.partition_broadcast(P)))
                    for h in range(2):
                        loads.append((scales[:, k + 1, :, h * HALF:(h + 1) * HALF],
                                      src[:, (1 - h) * HALF:(2 - h) * HALF].partition_broadcast(P)))
                for k in range(FK):
                    for at, off in ((B_VAL, 0), (B_GATE, FF)):
                        loads.append((par_all[0:FROWS[k], :, at + k],
                                      b1[:, off + k * P:off + k * P + FROWS[k]].rearrange("l p -> p l")))
                for at, src in ((B_G, ln_g), (B_B, ln_b), (B_B2, b2)):
                    loads.append((par_all[:, :, at], src.rearrange("l p -> p l")))
                sp.wait_ge(f_par, 1)
                with nc.allow_non_contiguous_dma(reason="a few per-feature parameters"):
                    for dst, src in loads:
                        sp.dma_start(dst, src).then_inc(loaded, 16)
                sp.wait_ge(loaded, 32 + 16 * len(loads))
                sp.wait_ge(w_att, 32)

            @block.vector
            def _(dve):
                nc.vector.memset(v2[:, :, :, :, :, :], 0.0)

            @block.gpsimd
            def _(pool):
                nc.gpsimd.memset(kb[:, :, :, :, :], 0.0)
                nc.gpsimd.memset(vtok[:, :, :, :, :], 0.0)
                nc.gpsimd.memset(par_all[:, :, :], 0.0).then_inc(f_par, 1)
                pool.wait_ge(loaded, 32 + 16 * 15)
                make_tables(pool, 0, f_tab)

        with nc.Fori(0, DEPTH) as layer:
            with ExitStack() as scope:
                xs = sb("xs", [P, P], scope=scope)
                raw = sb("raw", [P, 2, 2, UH, DH], scope=scope)
                sq = sb("sq", [P, 2 * UW], scope=scope)
                ss0, ss = sb("ss0", [P, 2 * UH], scope=scope), sb("ss", [P, 2, 2 * UH], scope=scope)
                lns, r0 = sb("lns", [P, 2 * UH], scope=scope), sb("r0", [P, 2, 2 * UH], scope=scope)
                r1, r = sb("r1", [P, 2 * UH], scope=scope), sb("r", [P, 2, 2 * UH], scope=scope)
                rc = sb("rc", [P, 2, 2, UH, DH], scope=scope)
                rs = sb("rs", [P, 2, UH, DH], scope=scope)
                qkn = sb("qkn", [P, 2, 2, UH, DH], scope=scope)
                qT = sb("qT", [P, 2, UP, P], scope=scope)
                sm = sb("sm", [P, 2, UH], scope=scope)
                sub = sb("sub", [P, UH, 2 * WIN], scope=scope)
                e = sb("e", [P, 2, UH, 2 * WIN], scope=scope)
                den, rden = sb("den", [P, UH], scope=scope), sb("rden", [P, 2, UH], scope=scope)
                pT = sb("pT", [P, 2, UP, P], scope=scope)
                o = sb("o", [P, 2, UH, DH], scope=scope)
                oT = sb("oT", [P, 2, UP, P], scope=scope)
                bA, bT, bS, bO, bX, bY = bank[0:2], bank[2:4], bank[4], bank[5], bank[6], bank[7]
                with nc.Block() as block:
                    @block.sync
                    def _(sp):
                        sp.dma_start(w1_sb[:, :], w1[ds(layer, 1), :, :].rearrange("l p n -> (l p) n")).then_inc(w_ffn, 16)
                        sp.dma_start(w2_sb[:, 0:2, :], w2[ds(layer, 1), 0:2 * P, :].rearrange(
                            "l (c p) n -> (l p) c n", p=P)).then_inc(w_ffn, 16)
                        sp.dma_start(w2_sb[0:FROWS[2], 2, :], w2[ds(layer, 1), 2 * P:FF, :].rearrange(
                            "l p n -> (l p) n")).then_inc(w_ffn, 16)

                        def step(at):
                            u = at(0)
                            if u and u.half == 1:
                                sp.wait_ge(v_raw, upto(u.g))
                                for hp in range(2):
                                    rows = hp * 64
                                    tok, by_win = vtok[:, u.slot, hp, :, :], v2[:, u.slot, :, hp, :, :]
                                    sp.dma_start(by_win[rows:rows + WIN, 0, :, :], vtok[P - WIN:P, 1 - u.slot, hp, :, :])\
                                        .then_inc(v2_ready[u.slot], 16)
                                    sp.dma_start(by_win[rows + WIN:rows + 2 * WIN, 0, :, :], tok[0:WIN, :, :])\
                                        .then_inc(v2_ready[u.slot], 16)
                                    for w in range(1, WINS):
                                        sp.dma_start(by_win[rows:rows + 2 * WIN, w, :, :], tok[(w - 1) * WIN:(w + 1) * WIN, :, :])\
                                            .then_inc(v2_ready[u.slot], 16)
                        run_steps(sp, layer, step, UNITS, ATT_LAG, 4, 2)

                    @block.gpsimd
                    def _(pool):
                        def step(at):
                            u = at(0)
                            if u and u.half == 0:
                                pool.wait_ge(v_mm, upto(u.g - 1))
                                pool.wait_ge(sin_done, upto(u.g - 1))
                                pool.sem_inc(xs_begun, 1)
                                nc.gpsimd.tensor_copy(xs[0:64, :], xa[0:64, ds(col(u.tile), P)]).then_inc(xs_ready, 1)
                                nc.gpsimd.tensor_copy(xs[64:P, :], xa[64:P, ds(col(u.tile) - 1, P)]).then_inc(xs_ready, 1)
                                pool.wait_ge(xs_ready, upto(u.g) + 1)
                            u = at(1)
                            if u:
                                h = u.half
                                pool.wait_ge(r_ready, upto(u.g))
                                pool.wait_ge(rot_ready, upto(u.g))
                                pool.wait_ge(kT_mm, upto(u.g - 2))
                                for k, done in enumerate((qn_ready, kn_ready)):
                                    nc.gpsimd.tensor_tensor(qkn[:, h, k, :, :], rc[:, h, k, :, :],
                                                            r[:, h, k * UH:(k + 1) * UH].unsqueeze(2).broadcast_to([P, UH, DH]),
                                                            ALU.mult).then_inc(done, 1)
                            u = at(0)
                            if u:
                                h = u.half
                                pool.wait_ge(f_tab, 4)
                                pool.wait_ge(q_raw, upto(u.g))
                                pool.wait_ge(k_raw, upto(u.g))
                                pool.wait_ge(rot_ready, upto(u.g - 1))
                                tt = pool.snap(u.tile % BT) if not isinstance(u.tile, int) else u.tile % BT
                                for hf in range(2):
                                    last = nc.gpsimd.tensor_tensor(
                                        rs[:, :, :, hf * HALF:(hf + 1) * HALF],
                                        raw[:, h, :, :, (1 - hf) * HALF:(2 - hf) * HALF],
                                        tab[:, 1::2, ds(tt, 1), hf * HALF:(hf + 1) * HALF].broadcast_to([P, 2, UH, HALF]),
                                        ALU.mult)
                                last.then_inc(sin_done, 1)
                        run_steps(pool, layer, step, UNITS, ATT_LAG, 4, 2)

                    @block.scalar
                    def _(act):
                        nc.scalar.preload_act_table_set("natural_log_exp_and_others")

                        def step(at):
                            u = at(0)
                            if u:
                                h = u.half
                                act.wait_ge(cos_done, upto(u.g - 2))
                                act.wait_ge(sin_done, upto(u.g - 2))
                                act.wait_ge(ss_sum, upto(u.g - 1))
                                act.wait_ge(q_mm, upto(u.g))
                                nc.scalar.copy(raw[:, h, 0, :, :], bA[h][:, :].rearrange("p (h d) -> p h d", d=DH)).then_inc(q_raw, 1)
                                nc.scalar.activation(sq[:, 0:UW], bA[h][:, :], ACT.Square).then_inc(q_sq, 1)
                                act.wait_ge(k_mm, upto(u.g))
                                nc.scalar.copy(raw[:, h, 1, :, :], bA[1 - h][:, :].rearrange("p (h d) -> p h d", d=DH)).then_inc(k_raw, 1)
                                nc.scalar.activation(sq[:, UW:2 * UW], bA[1 - h][:, :], ACT.Square).then_inc(k_sq, 1)
                            u = at(4)
                            if u:
                                act.wait_ge(oT_mm, upto(u.g))
                                act.wait_ge(y_mm, upto(u.g - 2))
                                nc.scalar.copy(oT[:, u.half, :, :], bX[:, :].rearrange("p (a c) -> p a c", a=UP))\
                                    .then_inc(oT_ready, 1)
                            u = at(0)
                            if u:
                                h = u.half
                                act.wait_ge(v_mm, upto(u.g))
                                act.wait_ge(v2_ready[u.slot], V2_LEAD + V2_TILE * ((u.tg - u.slot) // 2))
                                act.wait_ge(v2_ready[1 - u.slot], V2_LEAD + V2_TILE * ((u.tg + u.slot) // 2))
                                if h == 1:
                                    act.wait_ge(av_mm, upto(u.g - 4))
                                nc.scalar.copy(vtok[:, u.slot, :, h, :], bA[h][:, :].rearrange("p (a c) -> p a c", a=2))\
                                    .then_inc(v_raw, 1)
                            u = at(1)
                            if u:
                                act.wait_ge(qT_mm, upto(u.g))
                                act.wait_ge(s_mm, upto(u.g - 2))
                                nc.scalar.copy(qT[:, u.half, :, :], bT[0][:, :].rearrange("p (a c) -> p a c", a=UP))\
                                    .then_inc(qT_ready, 1)
                            u = at(1)
                            if u:
                                act.wait_ge(halo_ready, upto(u.g))
                                act.wait_ge(kT_mm, upto(u.g))
                                for hp in range(2):
                                    rows = slice(64 * hp, 64 * hp + 64)
                                    last = nc.scalar.copy(kb[rows, u.half, :, hp, WIN:WIN + P],
                                                          bT[1][rows, :].rearrange("p (a c) -> p a c", a=UP))
                                last.then_inc(kb_ready, 1)
                            u = at(2)
                            if u:
                                act.wait_ge(sub_done, upto(u.g))
                                act.wait_ge(pT_mm, upto(u.g - 2))
                                act.wait_ge(den_done, upto(u.g - 2))
                                nc.scalar.activation(e[:, u.half, :, :], sub[:, :, :], ACT.Exp).then_inc(e_ready, 1)
                            u = at(0)
                            if u:
                                act.wait_ge(ss_ready, upto(u.g))
                                nc.scalar.activation(lns[:, :], ss[:, u.half, :], ACT.Ln, scale=R_SCALE ** 2)\
                                    .then_inc(ln_done, 1)
                                act.wait_ge(ln_done, upto(u.g))
                                nc.scalar.activation(r0[:, u.half, :], lns[:, :], ACT.Exp, scale=-0.5).then_inc(r0_ready, 1)
                            u = at(0)
                            if u:
                                act.wait_ge(s_mm, upto(u.g - 2))
                                act.wait_ge(kb_ready, upto(u.g - 2))
                                for hp in range(2):
                                    rows = slice(64 * hp, 64 * hp + 64)
                                    last = nc.scalar.activation(kb[rows, u.half, :, hp, 0:WIN], kb[rows, u.half, :, hp, P:P + WIN],
                                                                ACT.Copy, scale=halo_decay[rows, :])
                                last.then_inc(halo_ready, 1)
                            u = at(2)
                            if u:
                                act.wait_ge(pT_mm, upto(u.g))
                                act.wait_ge(av_mm, upto(u.g - 2))
                                nc.scalar.copy(pT[:, u.half, :, :], bX[:, :].rearrange("p (a c) -> p a c", a=UP))\
                                    .then_inc(pT_ready, 1)
                        run_steps(act, layer, step, UNITS, ATT_LAG, 4, 2)

                    @block.vector
                    def _(dve):
                        def step(at):
                            u = at(2)
                            if u:
                                s = bS[:, :].rearrange("p (h c) -> p h c", c=2 * WIN)
                                dve.wait_ge(s_mm, upto(u.g))
                                dve.wait_ge(sub_done, upto(u.g - 2))
                                nc.vector.tensor_reduce(sm[:, u.half, :], s, AX.X, ALU.max).then_inc(max_done, 1)
                                dve.wait_ge(max_done, upto(u.g))
                                dve.wait_ge(e_ready, upto(u.g - 1))
                                nc.vector.tensor_tensor(sub[:, :, :], s, sm[:, u.half, :].unsqueeze(2).broadcast_to([P, UH, 2 * WIN]),
                                                        ALU.subtract).then_inc(sub_done, 1)
                            u = at(0)
                            if u:
                                h = u.half
                                dve.wait_ge(q_raw, upto(u.g))
                                dve.wait_ge(k_raw, upto(u.g))
                                dve.wait_ge(kn_ready, upto(u.g - 2))
                                tt = u.tile % BT
                                nc.vector.tensor_tensor(rc[:, h, :, :, :], raw[:, h, :, :, :],
                                                        tab[:, 0::2, ds(tt, 1), :].broadcast_to([P, 2, UH, DH]),
                                                        ALU.mult).then_inc(cos_done, 1)
                            u = at(0)
                            if u:
                                dve.wait_ge(k_sq, upto(u.g))
                                dve.wait_ge(q_sq, upto(u.g))
                                dve.wait_ge(ss_ready, upto(u.g - 1))
                                nc.vector.tensor_reduce(ss0[:, :], sq[:, :].rearrange("p (h d) -> p h d", d=DH), AX.X, ALU.add)\
                                    .then_inc(ss_sum, 1)
                                dve.wait_ge(ss_sum, upto(u.g))
                                dve.wait_ge(nt_half, upto(u.g - 2))
                                nc.vector.tensor_scalar(ss[:, u.half, :], ss0[:, :], 1e-24, None, ALU.max).then_inc(ss_ready, 1)
                            u = at(3)
                            if u:
                                dve.wait_ge(av_mm, upto(u.g))
                                dve.wait_ge(rden_ready, upto(u.g))
                                dve.wait_ge(oT_mm, upto(u.g - 2))
                                nc.vector.tensor_tensor(o[:, u.half, :, :], bO[:, :].rearrange("p (h d) -> p h d", d=DH),
                                                        rden[:, u.half, :].unsqueeze(2).broadcast_to([P, UH, DH]),
                                                        ALU.mult).then_inc(o_ready, 1)
                            u = at(0)
                            if u:
                                h = u.half
                                dve.wait_ge(sin_done, upto(u.g))
                                dve.wait_ge(cos_done, upto(u.g))
                                nc.vector.tensor_tensor(rc[:, h, :, :, :], rc[:, h, :, :, :], rs[:, :, :, :], ALU.add)\
                                    .then_inc(rot_ready, 1)
                            u = at(0)
                            if u:
                                h = u.half
                                dve.wait_ge(r0_ready, upto(u.g))
                                dve.wait_ge(nt_half, upto(u.g - 1))
                                dve.wait_ge(r_ready, upto(u.g - 1))
                                nc.vector.tensor_tensor(r1[:, :], r0[:, h, :], r0[:, h, :], ALU.mult).then_inc(nt_sq, 1)
                                dve.wait_ge(nt_sq, upto(u.g))
                                nc.vector.scalar_tensor_tensor(out=r1[:, :], in0=r1[:, :], scalar=-0.5 * R_SCALE ** 2,
                                                               in1=ss[:, h, :], op0=ALU.mult, op1=ALU.mult).then_inc(nt_half, 1)
                                dve.wait_ge(nt_half, upto(u.g))
                                dve.wait_ge(qn_ready, upto(u.g - 2))
                                dve.wait_ge(kn_ready, upto(u.g - 2))
                                nc.vector.scalar_tensor_tensor(out=r[:, h, :], in0=r1[:, :], scalar=1.5, in1=r0[:, h, :],
                                                               op0=ALU.add, op1=ALU.mult).then_inc(r_ready, 1)
                            u = at(4)
                            if u and u.half == 1:
                                dve.wait_ge(y_mm, upto(u.g))
                                nc.vector.tensor_tensor(xb[:, ds(col(u.tile), P)], bY[:, 0:P], xa[:, ds(col(u.tile), P)],
                                                        ALU.add).then_inc(y_used, 1)
                            u = at(2)
                            if u:
                                dve.wait_ge(e_ready, upto(u.g))
                                dve.wait_ge(rden_ready, upto(u.g - 1))
                                nc.vector.tensor_reduce(den[:, :], e[:, u.half, :, :], AX.X, ALU.add).then_inc(den_done, 1)
                                dve.wait_ge(den_done, upto(u.g))
                                dve.wait_ge(o_ready, upto(u.g - 2))
                                nc.vector.reciprocal(rden[:, u.half, :], den[:, :]).then_inc(rden_ready, 1)
                        run_steps(dve, layer, step, UNITS, ATT_LAG, 4, 2)

                    @block.tensor
                    def _(pe):
                        def step(at):
                            u = at(0)
                            if u:
                                h = u.half
                                if h == 0:
                                    pe.wait_ge(w_att, 32 * layer + 32)
                                    pe.wait_ge(xs_ready, upto(u.g) + 1)
                                pe.wait_ge(k_sq, upto(u.g - 1))
                                nc.tensor.matmul(bA[h][:, :], xs[:, :], wqkv_sb[:, h * UW:(h + 1) * UW],
                                                 start=True, stop=True).then_inc(q_mm, 1)
                                pe.wait_ge(v_raw, upto(u.g - 1))
                                nc.tensor.matmul(bA[1 - h][:, :], xs[:, :], wqkv_sb[:, INNER + h * UW:INNER + (h + 1) * UW],
                                                 start=True, stop=True).then_inc(k_mm, 1)
                            u = at(4)
                            if u:
                                pe.wait_ge(o_ready, upto(u.g))
                                if at(3):
                                    pe.wait_ge(pT_ready, upto(at(3).g))
                                for c in range(UP):
                                    last = nc.tensor.transpose(bX[:, c * P:(c + 1) * P], o[:, u.half, 2 * c:2 * c + 2, :]
                                                               .rearrange("p a d -> p (a d)"), ident)
                                last.then_inc(oT_mm, 1)
                            u = at(0)
                            if u:
                                h = u.half
                                pe.wait_ge(q_sq, upto(u.g))
                                wv = wqkv_sb[:, 2 * INNER + h * UW:2 * INNER + (h + 1) * UW]
                                nc.tensor.matmul(bA[h][:, :], xs[:, :], wv.rearrange("p (c a d) -> p a c d", a=2, d=DH),
                                                 start=True, stop=True).then_inc(v_mm, 1)
                            u = at(1)
                            if u:
                                pe.wait_ge(kn_ready, upto(u.g))
                                for k, (free, done) in enumerate(((qT_ready, qT_mm), (kb_ready, kT_mm))):
                                    pe.wait_ge(free, upto(u.g - 1))
                                    for c in range(UP):
                                        last = nc.tensor.transpose(bT[k][:, c * P:(c + 1) * P], qkn[:, u.half, k, 2 * c:2 * c + 2, :]
                                                                   .rearrange("p a d -> p (a d)"), ident)
                                    last.then_inc(done, 1)
                            u = at(3)
                            if u:
                                pe.wait_ge(pT_ready, upto(u.g))
                                pe.wait_ge(v2_ready[u.slot], V2_LEAD + V2_TILE * ((u.tg - u.slot) // 2 + 1))
                                pe.wait_ge(o_ready, upto(u.g - 1))
                                for c in range(UP):
                                    for w in range(WINS):
                                        last = nc.tensor.matmul(
                                            bO[w * WIN:(w + 1) * WIN, c * P:(c + 1) * P], pT[:, u.half, c, w * WIN:(w + 1) * WIN],
                                            v2[:, u.slot, w, :, u.half, c * DH:(c + 1) * DH], start=True, stop=True)
                                last.then_inc(av_mm, 1)
                            u = at(4)
                            if u:
                                pe.wait_ge(oT_ready, upto(u.g))
                                if u.half == 0:
                                    pe.wait_ge(y_used, upto(u.tg - 1))
                                for c in range(UP):
                                    last = nc.tensor.matmul(bY[:, 0:P], wo_sb[:, u.half * UP + c, :], oT[:, u.half, c, :],
                                                            start=(u.half == 0 and c == 0), stop=(u.half == 1 and c == UP - 1))
                                last.then_inc(y_mm, 1)
                            u = at(1)
                            if u:
                                pe.wait_ge(qT_ready, upto(u.g))
                                pe.wait_ge(kb_ready, upto(u.g))
                                pe.wait_ge(sub_done, upto(u.g - 1))
                                later = (u.tile % BT + BT - 1) // BT
                                nc.tensor.matmul(bS[:, :], identb[:, :], mask[:, ds(later * UW, UW)], start=True, stop=True)
                                for c in range(UP):
                                    for w in range(WINS):
                                        last = nc.tensor.matmul(
                                            bS[w * WIN:(w + 1) * WIN, c * P:(c + 1) * P], qT[:, u.half, c, w * WIN:(w + 1) * WIN],
                                            kb[:, u.half, c, :, w * WIN:w * WIN + 2 * WIN], start=False,
                                            stop=True, skip_group_check=True)
                                last.then_inc(s_mm, 1)
                            u = at(2)
                            if u:
                                pe.wait_ge(e_ready, upto(u.g))
                                pe.wait_ge(oT_ready, upto(u.g - 2))
                                for c in range(UP):
                                    last = nc.tensor.transpose(bX[:, c * P:(c + 1) * P], e[:, u.half, 2 * c:2 * c + 2, :]
                                                               .rearrange("p a d -> p (a d)"), ident)
                                last.then_inc(pT_mm, 1)
                        run_steps(pe, layer, step, UNITS, ATT_LAG, 4, 2)

            with ExitStack() as scope:
                xf = sb("xf", [P, 2, P], scope=scope)
                xt = sb("xt", [P, TILES, D], scope=scope)
                stats = sb("stats", [P, TILES, 6], scope=scope)
                small = sb("small", [P, 6, TILES], scope=scope)
                xn = sb("xn", [P, 2, 4, D], scope=scope)
                xnT = sb("xnT", [P, 2, CHUNK], scope=scope)
                ge = sb("ge", [P, 2, CHUNK], scope=scope)
                hb = sb("hb", [P, 2, FK, CHUNK], scope=scope)
                bN, bG, bV, bY = bank[0:2], bank[2:4], bank[4:6], bank[6:8]

                with nc.Block() as block:
                    @block.sync
                    def _(sp):
                        load_att_weights(sp, (layer + 1) % DEPTH)

                    @block.gpsimd
                    def _(pool):

                        def step(at):
                            u = at(0)
                            pool.wait_ge(f1_mm, upto(u.g - 2))
                            pool.wait_ge(f1_x, upto(u.g - 1))
                            nc.gpsimd.tensor_copy(xf[0:64, u.slot, :], xb[0:64, ds(col(u.tile), P)]).then_inc(f1_low, 1)
                            pool.wait_ge(f1_low, upto(u.g))
                            nc.gpsimd.tensor_copy(xf[64:P, u.slot, :], xb[64:P, ds(col(u.tile) - 1, P)]).then_inc(f1_x, 1)
                        run_steps(pool, layer, step, TILES, 0, 2, 1)
                        pool.wait_ge(f1_x, TILES * layer + TILES + LEAD)
                        make_tables(pool, (layer + 1) % DEPTH, f_tab)

                    @block.tensor
                    def _(pe):
                        def step(at):
                            u = at(0)
                            pe.wait_ge(f1_x, upto(u.g))
                            pe.wait_ge(f1_tok, upto(u.g - 2))
                            nc.tensor.transpose(bN[u.slot][:, 0:P], xf[:, u.slot, :], ident).then_inc(f1_mm, 1)
                        run_steps(pe, layer, step, TILES, 0, 2, 1)

                    @block.scalar
                    def _(act):
                        def step(at):
                            u = at(0)
                            act.wait_ge(f1_mm, upto(u.g))
                            nc.scalar.copy(xt[:, ds(u.tile, 1), :].rearrange("p a b -> p (a b)"), bN[u.slot][:, 0:P]).then_inc(f1_tok, 1)
                        run_steps(act, layer, step, TILES, 0, 2, 1)
                        act.wait_ge(f_stat, (STATS + REFINE) * layer + STATS)
                        rsqrt_seed(act, small, f_ln, 2 * layer)

                    @block.vector
                    def _(dve):
                        def step(at):
                            u = at(0)
                            dve.wait_ge(f1_tok, upto(u.g))
                            nc.vector.bn_stats(stats[:, ds(u.tile, 1), :].rearrange("p a b -> p (a b)"),
                                               xt[:, ds(u.tile, 1), :].rearrange("p a b -> p (a b)")).then_inc(f1_stat, 1)
                        run_steps(dve, layer, step, TILES, 0, 2, 1)
                        nc.vector.tensor_copy(par[:, :], par_all[:, ds(layer, 1), :].rearrange("p a b -> p (a b)"))
                        dve.wait_ge(f1_stat, TILES * layer + TILES + LEAD)
                        finish_stats(dve, stats, small, f_stat, (STATS + REFINE) * layer)
                        dve.wait_ge(f_ln, 2 * layer + 2)
                        rsqrt_refine(dve, small, f_stat, (STATS + REFINE) * layer + STATS)

                with nc.Block() as block:
                    @block.vector
                    def _(dve):
                        def step(at):
                            u = at(0)
                            if u:
                                dve.wait_ge(f2_tr, upto(u.g - 2))
                                for j in range(4):
                                    t = u.tile * 4 + j
                                    last = nc.vector.tensor_scalar(xn[:, u.slot, j, :], xt[:, ds(t, 1), :].rearrange("p a b -> p (a b)"),
                                                                   small[:, 0, ds(t, 1)], small[:, 4, ds(t, 1)],
                                                                   ALU.subtract, ALU.mult)
                                last.then_inc(f2_norm, 1)
                            u = at(1)
                            if u:
                                for k in range(FK):
                                    n, b = FROWS[k], (u.slot * FK + k) % 2
                                    dve.wait_ge(f2_gelu, FLEAD + FK * u.g + k + 1)
                                    dve.wait_ge(f2_val, FLEAD + FK * u.g + k + 1)
                                    dve.wait_ge(f2_y, upto(u.g - 2))
                                    nc.vector.scalar_tensor_tensor(
                                        out=hb[0:n, u.slot, k, :], in0=bV[b][0:n, :], scalar=par[0:n, B_VAL + k:B_VAL + k + 1],
                                        in1=ge[0:n, b, :], op0=ALU.add, op1=ALU.mult).then_inc(f2_h, 1)
                            u = at(2)
                            if u:
                                dve.wait_ge(f2_y, upto(u.g))
                                c = u.tile * CHUNK + u.tile // (CHUNKS // BATCH) + 1
                                nc.vector.scalar_tensor_tensor(
                                    out=xa[:, ds(c, CHUNK)], in0=bY[u.slot][:, :], scalar=par[:, B_B2:B_B2 + 1],
                                    in1=xb[:, ds(c, CHUNK)], op0=ALU.add, op1=ALU.add).then_inc(f2_res, 1)
                        run_steps(dve, layer, step, CHUNKS, FFN_LAG, 2, 1)

                    @block.scalar
                    def _(act):
                        def step(at):
                            u = at(0)
                            if u:
                                act.wait_ge(f2_tr, upto(u.g))
                                act.wait_ge(f2_val, FLEAD + FK * (u.g - 1))
                                nc.scalar.activation(xnT[:, u.slot, :], bN[u.slot][:, :], ACT.Identity,
                                                     scale=par[:, B_G:B_G + 1], bias=par[:, B_B:B_B + 1]).then_inc(f2_xT, 1)
                            u = at(1)
                            if u:
                                for k in range(FK):
                                    n, b = FROWS[k], (u.slot * FK + k) % 2
                                    act.wait_ge(f2_gate, FLEAD + FK * u.g + k + 1)
                                    act.wait_ge(f2_h, FLEAD + FK * u.g + k - 1)
                                    nc.scalar.activation(ge[0:n, b, :], bG[b][0:n, :], ACT.Gelu,
                                                         bias=par[0:n, B_GATE + k:B_GATE + k + 1]).then_inc(f2_gelu, 1)
                        run_steps(act, layer, step, CHUNKS, FFN_LAG, 2, 1)

                    @block.tensor
                    def _(pe):
                        def step(at):
                            u = at(2)
                            if u:
                                pe.wait_ge(f2_res, upto(u.g - 2))
                                for k in range(FK):
                                    pe.wait_ge(f2_h, FLEAD + FK * u.g + k + 1)
                                    last = nc.tensor.matmul(bY[u.slot][:, :], w2_sb[0:FROWS[k], k, :], hb[0:FROWS[k], u.slot, k, :],
                                                            start=(k == 0), stop=(k == FK - 1))
                                last.then_inc(f2_y, 1)
                            u = at(0)
                            if u:
                                pe.wait_ge(f2_norm, upto(u.g))
                                pe.wait_ge(f2_xT, upto(u.g - 2))
                                for j in range(4):
                                    last = nc.tensor.transpose(bN[u.slot][:, j * P:(j + 1) * P], xn[:, u.slot, j, :], ident)
                                last.then_inc(f2_tr, 1)
                            u = at(1)
                            if u:
                                pe.wait_ge(w_ffn, 48 * layer + 48)
                                pe.wait_ge(f2_xT, upto(u.g))
                                for k in range(FK):
                                    n, b = FROWS[k], (u.slot * FK + k) % 2
                                    pe.wait_ge(f2_gelu, FLEAD + FK * u.g + k - 1)
                                    nc.tensor.matmul(bG[b][0:n, :], w1_sb[:, FF + k * P:FF + k * P + n], xnT[:, u.slot, :],
                                                     start=True, stop=True).then_inc(f2_gate, 1)
                                    pe.wait_ge(f2_h, FLEAD + FK * u.g + k - 1)
                                    nc.tensor.matmul(bV[b][0:n, :], w1_sb[:, k * P:k * P + n], xnT[:, u.slot, :],
                                                     start=True, stop=True).then_inc(f2_val, 1)
                        run_steps(pe, layer, step, CHUNKS, FFN_LAG, 2, 1)

        with ExitStack() as scope:
            att = sb("att", [P, TILES, D], scope=scope)
            xf = sb("xf_end", [P, 2, P], scope=scope)
            GROUP = 8
            with nc.Block() as block:
                @block.sync
                def _(sp):
                    sp.dma_start(att[:, :, :], att_src.rearrange("(n p) d -> p n d", p=P)).then_inc(fin_in, 16)
                    dst = out.rearrange("b (n p) d -> p (b n) d", p=P)
                    for n in range(TILES // GROUP):
                        sp.wait_ge(fin_add, 1 + GROUP * (n + 1))
                        sp.dma_start(dst[:, n * GROUP:(n + 1) * GROUP, :], att[:, n * GROUP:(n + 1) * GROUP, :])\
                            .then_inc(fin_out, 16)
                    sp.wait_ge(w_att, 32 * (DEPTH + 1))
                    sp.wait_ge(fin_out, 16 * (TILES // GROUP))

                @block.gpsimd
                def _(pool):
                    with pool.Fori(0, TILES // 2) as i:
                        for e in range(2):
                            t = 2 * i + e
                            pool.wait_ge(fin_mm, 1 + 2 * i)
                            nc.gpsimd.tensor_copy(xf[:, e, :], xa[:, ds(col(t), P)]).then_inc(fin_x, 1)

                @block.tensor
                def _(pe):
                    with pe.Fori(0, TILES // 2) as i:
                        for e in range(2):
                            t = 2 * i + e
                            pe.wait_ge(fin_x, t + 1)
                            pe.wait_ge(fin_add, 1 + 2 * i)
                            nc.tensor.transpose(bank[e][:, 0:P], xf[:, e, :], ident).then_inc(fin_mm, 1)

                @block.vector
                def _(dve):
                    dve.wait_ge(fin_in, 16)
                    with dve.Fori(0, TILES // 2) as i:
                        for e in range(2):
                            t = 2 * i + e
                            dve.wait_ge(fin_mm, t + 2)
                            a = att[:, ds(t, 1), :].rearrange("p a b -> p (a b)")
                            nc.vector.tensor_tensor(a, bank[e][:, 0:P], a, ALU.add).then_inc(fin_add, 1)


_INS = ["L0_attn_hidden_states", "L0_attn_Wqkv", "L0_attn_bqkv", "L0_attn_Wout", "L0_attn_bout", "L0_ffn_Wqkv",
        "L0_ffn_q_scale", "L0_ffn_k_scale", "L0_ffn_Wo", "L0_ffn_ln_g", "L0_ffn_ln_b", "L0_ffn_W1", "L0_ffn_b1",
        "L0_ffn_W2", "L0_ffn_b2"]


def kernel(**inputs):
    import concourse.bacc as bacc
    from concourse.bass_utils import run_bass_kernel_spmd

    nc = bacc.Bacc("TRN2", target_bir_lowering=False, num_devices=1)
    arrays, args = {}, []
    for name, a in [(n, np.ascontiguousarray(inputs[n])) for n in _INS] + [("constants", constants())]:
        arrays[f"in_{name}"] = a
        args.append(nc.dram_tensor(f"in_{name}", a.shape, mybir.dt.from_np(a.dtype), kind="ExternalInput").ap())
    args.append(nc.dram_tensor("out_x", (BATCH, SEQ, D), mybir.dt.float32, kind="ExternalOutput").ap())
    program(nc, *args)
    r = run_bass_kernel_spmd(nc, [arrays], core_ids=[0])
    return r.results[0]["out_x"]
```

```python
import math
from collections import namedtuple
from contextlib import ExitStack

import numpy as np
import concourse.bass as bass
from concourse import mybir

P = 128
BATCH, SEQ, D = 2, 2048, 128
TOK = BATCH * SEQ
TILES = TOK // P
BT = SEQ // P
DEPTH, HEADS, DH = 6, 16, 64
INNER = HEADS * DH
WIN = 32
WINS = P // WIN
HALF = DH // 2
QK_SCALE = 8.0
FF = int(D * 4 * 2 / 3)
FK = 3
FROWS = [P, P, FF - 2 * P]
XCOLS = SEQ + 1
NH, NDH, NM = 16, 8, 64
NL = SEQ // NM
PINV_ITERS = 6
PAIRS = NH // 2
EPS = 1e-5

UH = HEADS // 2
UW = UH * DH
UP = UH // 2
UNITS = 2 * TILES
ATT_LAG = 8
CHUNK = 4 * P
CHUNKS = TOK // CHUNK
FFN_LAG = 4
LEAD = 4
FLEAD = 2 * FK
QLEAD = 4 * LEAD
R_SCALE = 256.0
MASKED = -1e30
V2_TILE = 16 * 2 * WINS
V2_TAIL = 16 * 2
V2_LEAD = 16

C_ROT = 0
C_MASK = C_ROT + 4 * BT * DH
C_IDENT = C_MASK + 2 * UW
C_HALO = C_IDENT + P
C_HEAD = C_HALO + 1
C_PAIR = C_HEAD + NH
C_ALL = C_PAIR + 2 * NDH

B_VAL, B_GATE, B_G, B_B, B_B2, B_ALL = 0, FK, 2 * FK, 2 * FK + 1, 2 * FK + 2, 2 * FK + 3

Unit = namedtuple("Unit", "g half slot tile tg")


def constants():
    half = np.arange(0, DH, 2, dtype=np.float32)
    inv_freq = (1.0 / (np.float32(10000.0) ** (half / np.float32(DH)))).astype(np.float32)
    t = np.arange(SEQ, dtype=np.float32)
    ang = (t[:, None] * inv_freq[None, :]).astype(np.float32).astype(np.float64)
    base = (half.astype(np.float64) + 0.4 * DH) / (1.4 * DH)
    power = ((np.arange(SEQ) % P) - P // 2) / (WIN // 2)
    sc = base[None, :] ** power[:, None]
    cos, sin, sc = (np.concatenate([a, a], -1) for a in (np.cos(ang), np.sin(ang), sc))
    sin[:, :HALF] *= -1.0
    c = np.zeros((P, C_ALL), np.float32)
    for k, tab in enumerate([cos * sc * QK_SCALE, sin * sc * QK_SCALE, cos / sc, sin / sc]):
        a = (tab * R_SCALE).reshape(BT, P, DH).transpose(1, 0, 2).reshape(P, BT * DH)
        c[:, C_ROT + k * BT * DH:C_ROT + (k + 1) * BT * DH] = a
    q = np.arange(P)[:, None] % WIN
    k = np.arange(2 * WIN)[None, :]
    outside = (k < q) | (k > q + WIN)
    first = outside | ((np.arange(P)[:, None] < WIN) & (k < WIN))
    for n, m in enumerate((first, outside)):
        c[:, C_MASK + n * UW:C_MASK + (n + 1) * UW] = np.tile(np.where(m, MASKED, 0.0), (1, UH))
    c[:, C_IDENT:C_IDENT + P] = np.eye(P)
    c[:, C_HALO] = np.tile(base, 4) ** (P / (WIN // 2))
    c[:, C_HEAD:C_HEAD + NH] = np.arange(P)[:, None] // NDH == np.arange(NH)[None, :]
    c[:, C_PAIR:C_ALL] = np.arange(P)[:, None] // NM == np.arange(2 * NDH)[None, :] // NDH
    return c


def upto(n):
    return n + 1 + LEAD


def col(tile):
    return tile * P + tile // BT + 1


def run_steps(eng, layer, step, n_units, lag, unroll, per_tile):
    first = eng.snap(layer * n_units)
    first_tile = eng.snap(layer * (n_units // per_tile))

    def static(s):
        def at(k):
            u = s - k
            if not 0 <= u < n_units:
                return None
            t = u // per_tile
            return Unit(first + u, u % per_tile, t % 2, t, first_tile + t)
        return at

    for s in range(lag):
        step(static(s))
    with eng.Fori(0, (n_units - lag) // unroll) as i:
        now = eng.snap(first + unroll * i)
        tile = eng.snap((unroll // per_tile) * i)
        now_tile = eng.snap(first_tile + (unroll // per_tile) * i)
        for e in range(unroll):
            def at(k, e=e):
                u = lag + e - k
                t = u // per_tile
                return Unit(now + u, u % per_tile, t % 2, tile + t, now_tile + t)
            step(at)
    for s in range(n_units, n_units + lag):
        step(static(s))


def program(nc, hid, a_wqkv, a_bqkv, a_wout, a_bout, wqkv, q_scale, k_scale, wo, ln_g, ln_b, w1, b1, w2, b2,
            const, out):
    fp32, bf16 = mybir.dt.float32, mybir.dt.bfloat16
    ALU, ACT, AX = mybir.AluOpType, mybir.ActivationFunctionType, mybir.AxisListType
    ds = bass.ds
    part = mybir.dt.float32r

    ctx = ExitStack()
    with ctx:
        def sb(name, shape, dt=fp32, scope=ctx):
            return scope.enter_context(nc.sbuf_tensor(name, shape, dt))

        def sem(name):
            return ctx.enter_context(nc.semaphore(name))

        counted = []

        def csem(name):
            counted.append(sem(name))
            return counted[-1]

        psum = ctx.enter_context(nc.psum_tensor("psum", [P, 8 * 512], fp32))
        bank = [psum[:, i * 512:(i + 1) * 512] for i in range(8)]

        xa = sb("xa", [P, BATCH * XCOLS])
        consts = sb("consts", [P, C_ALL])
        rot = consts[:, C_ROT:C_MASK].rearrange("p (k t d) -> p k t d", k=4, t=BT)
        ident = consts[:, C_IDENT:C_IDENT + P]
        halo_decay = consts[:, C_HALO:C_HALO + 1]
        identb = sb("identb", [P, P], bf16)
        mask = sb("mask", [P, 2 * UW], bf16)

        a_k_mm, a_kT, a_v_mm, a_vT, a_vtr, a_v = (csem(n) for n in ("a_k_mm", "a_kT", "a_v_mm", "a_vT", "a_vtr", "a_v"))
        b_q, b_s, b_max, b_e, b_rs, b_z = (csem(n) for n in ("b_q", "b_s", "b_max", "b_e", "b_rs", "b_z"))
        b_tr, b_u = sem("b_tr"), sem("b_u")
        b_pT = [sem("b_pT_act"), sem("b_pT_dve")]
        (d_q, d_qT, d_s, d_max, d_sub, d_e, d_sum, d_rd, d_n, d_tr, d_pT, d_o, d_oT, d_y, d_add) = (csem(n) for n in (
            "d_q", "d_qT", "d_s", "d_max", "d_sub", "d_e", "d_sum", "d_rd", "d_n", "d_tr", "d_pT", "d_o", "d_oT", "d_y", "d_add"))

        xs_begun, xf_begun = sem("xs_begun"), sem("xf_begun")
        xs_high, xs_low = csem("xs_high"), csem("xs_low")
        xs_ready = csem("xs_ready")
        q_mm, k_mm, v_mm = csem("q_mm"), csem("k_mm"), csem("v_mm")
        q_raw, q_sq, k_raw, k_sq = (csem(n) for n in ("q_raw", "q_sq", "k_raw", "k_sq"))
        v_raw = csem("v_raw")
        ss_sum, ss_ready = csem("ss_sum"), csem("ss_ready")
        ln_done, r0_ready = csem("ln_done"), csem("r0_ready")
        nt_sq, nt_half, r_ready = csem("nt_sq"), csem("nt_half"), csem("r_ready")
        qn_ready, kn_ready = csem("qn_ready"), csem("kn_ready")
        cos_done, sin_done, rot_ready = csem("cos_done"), csem("sin_done"), csem("rot_ready")
        qT_mm, kT_mm = csem("qT_mm"), csem("kT_mm")
        qT_ready, halo_ready, kb_ready = csem("qT_ready"), csem("halo_ready"), csem("kb_ready")
        s_mm, max_done, sub_done, e_ready = (csem(n) for n in ("s_mm", "max_done", "sub_done", "e_ready"))
        den_done, rden_ready = csem("den_done"), csem("rden_ready")
        pT_mm, pT_ready, av_mm, o_ready = (csem(n) for n in ("pT_mm", "pT_ready", "av_mm", "o_ready"))
        oT_mm, oT_ready, y_mm = csem("oT_mm"), csem("oT_ready"), csem("y_mm")
        y_used = csem("y_used")
        v2_ready = [sem("v2_ready0"), sem("v2_ready1")]
        v2_tail = sem("v2_tail")
        f1_low = csem("f1_low")
        f1_x, f1_mm, f1_tok, f1_stat = (csem(n) for n in ("f1_x", "f1_mm", "f1_tok", "f1_stat"))
        f_stat = sem("f_stat")
        f_ln = sem("f_ln")
        f2_norm, f2_tr, f2_xT = csem("f2_norm"), csem("f2_tr"), csem("f2_xT")
        f2_low = csem("f2_low")
        w1_high, w1_low = sem("w1_high"), sem("w1_low")
        f2_gate, f2_val, f2_gelu, f2_h = (sem(n) for n in ("f2_gate", "f2_val", "f2_gelu", "f2_h"))
        f2_y, f2_res = csem("f2_y"), csem("f2_res")
        f_par, f_tab, w_att, w_ffn = sem("f_par"), sem("f_tab"), sem("w_att"), sem("w_ffn")
        split_turn = sem("split_turn")
        w_split = sem("w_split")
        fin_in, fin_x, fin_mm, fin_add, fin_out = (sem(n) for n in ("fin_in", "fin_x", "fin_mm", "fin_add", "fin_out"))
        x_in = [sem(f"x_in{n}") for n in range(4)]
        loaded, s_init, s_stat, s_ln, s_norm, s_tr, s_put = (
            sem(n) for n in ("loaded", "s_init", "s_stat", "s_ln", "s_norm", "s_tr", "s_put"))

        def finish_stats(dve, stats, small, count, base):
            mean, var, diff = small[:, 0, :], small[:, 1, :], small[:, 2, :]
            nc.vector.tensor_tensor(mean, stats[:, :, 1], stats[:, :, 4], ALU.add).then_inc(count, 1)
            nc.vector.tensor_tensor(diff, stats[:, :, 1], stats[:, :, 4], ALU.subtract).then_inc(count, 1)
            nc.vector.tensor_tensor(var, stats[:, :, 2], stats[:, :, 5], ALU.add).then_inc(count, 1)
            dve.wait_ge(count, base + 3)
            nc.vector.tensor_scalar(mean, mean, 0.5, None, ALU.mult).then_inc(count, 1)
            nc.vector.tensor_tensor(diff, diff, diff, ALU.mult).then_inc(count, 1)
            nc.vector.tensor_scalar(var, var, 1.0 / D, EPS, ALU.mult, ALU.add).then_inc(count, 1)
            dve.wait_ge(count, base + 6)
            nc.vector.scalar_tensor_tensor(out=var, in0=diff, scalar=0.25, in1=var, op0=ALU.mult,
                                           op1=ALU.add).then_inc(count, 1)

        def rsqrt_seed(act, small, count, base):
            nc.scalar.activation(small[:, 3, :], small[:, 1, :], ACT.Ln).then_inc(count, 1)
            act.wait_ge(count, base + 1)
            nc.scalar.activation(small[:, 4, :], small[:, 3, :], ACT.Exp, scale=-0.5).then_inc(count, 1)

        def rsqrt_refine(dve, small, count, base):
            var, sq, r = small[:, 1, :], small[:, 5, :], small[:, 4, :]
            nc.vector.tensor_tensor(sq, r, r, ALU.mult).then_inc(count, 1)
            dve.wait_ge(count, base + 1)
            nc.vector.scalar_tensor_tensor(out=sq, in0=sq, scalar=-0.5, in1=var, op0=ALU.mult,
                                           op1=ALU.mult).then_inc(count, 1)
            dve.wait_ge(count, base + 2)
            nc.vector.scalar_tensor_tensor(out=r, in0=sq, scalar=1.5, in1=r, op0=ALU.add,
                                           op1=ALU.mult).then_inc(count, 1)
        STATS, REFINE = 7, 3

        with ExitStack() as scope:
            xtok = sb("xtok", [P, TILES, D], scope=scope)
            stats = sb("stats0", [P, TILES, 6], scope=scope)
            small = sb("small0", [P, 6, TILES], scope=scope)
            xn = sb("xn0", [P, 2, 4, D], scope=scope)
            LOADS = 4
            PART = TILES // LOADS
            with nc.Block() as block:
                @block.sync
                def _(sp):
                    for n in range(LOADS):
                        part = slice(n * PART, (n + 1) * PART)
                        sp.dma_start(xtok[:, part, :], hid.rearrange("b (n p) d -> p (b n) d", p=P)[:, part, :]).then_inc(x_in[n], 16)
                    sp.dma_start(consts[:, :], const).then_inc(loaded, 16)
                    sp.wait_ge(loaded, 16)

                @block.gpsimd
                def _(pool):
                    for b in range(BATCH):
                        nc.gpsimd.memset(xa[:, b * XCOLS:b * XCOLS + 1], 0.0).then_inc(s_init, 1)
                    for s in counted:
                        pool.sem_inc(s, LEAD)
                    for s in (f2_gate, f2_val, f2_gelu, f2_h):
                        pool.sem_inc(s, FLEAD)
                    for s in (b_tr, b_u):
                        pool.sem_inc(s, QLEAD)
                    for s in b_pT:
                        pool.sem_inc(s, QLEAD // 2)
                    for s in (*v2_ready, v2_tail):
                        pool.sem_inc(s, V2_LEAD)
                    for s in (s_tr, s_put, fin_mm, fin_add):
                        pool.sem_inc(s, 1)

                @block.vector
                def _(dve):
                    for n in range(LOADS):
                        dve.wait_ge(x_in[n], 16)
                        for t in range(n * PART, (n + 1) * PART):
                            nc.vector.bn_stats(stats[:, t, :], xtok[:, t, :]).then_inc(s_stat, 1)
                    dve.wait_ge(s_stat, TILES)
                    finish_stats(dve, stats, small, s_stat, TILES)
                    dve.wait_ge(s_ln, 2)
                    rsqrt_refine(dve, small, s_norm, 0)
                    dve.wait_ge(s_norm, REFINE)
                    with dve.Fori(0, CHUNKS // 2) as i:
                        for e in range(2):
                            c = 2 * i + e
                            dve.wait_ge(s_tr, c + 1)
                            for j in range(4):
                                t = 4 * c + j
                                last = nc.vector.tensor_scalar(xn[:, e, j, :], xtok[:, ds(t, 1), :].rearrange("p a b -> p (a b)"),
                                                               small[:, 0, ds(t, 1)], small[:, 4, ds(t, 1)], ALU.subtract, ALU.mult)
                            last.then_inc(s_norm, 1)
                    dve.wait_ge(loaded, 16)
                    nc.vector.tensor_copy(identb[:, :], ident).then_inc(s_init, 1)
                    nc.vector.tensor_copy(mask[:, :], consts[:, C_MASK:C_IDENT]).then_inc(s_init, 1)

                @block.scalar
                def _(act):
                    nc.scalar.preload_act_table_set("natural_log_exp_and_others")
                    act.wait_ge(s_stat, TILES + STATS)
                    rsqrt_seed(act, small, s_ln, 0)
                    with act.Fori(0, CHUNKS // 2) as i:
                        for e in range(2):
                            c = 2 * i + e
                            act.wait_ge(s_tr, c + 2)
                            nc.scalar.copy(xa[:, ds(c * CHUNK + c // (CHUNKS // BATCH) + 1, CHUNK)], bank[e][:, :]).then_inc(s_put, 1)

                @block.tensor
                def _(pe):
                    pe.wait_ge(loaded, 16)
                    with pe.Fori(0, CHUNKS // 2) as i:
                        for e in range(2):
                            c = 2 * i + e
                            pe.wait_ge(s_norm, REFINE + c + 1)
                            pe.wait_ge(s_put, c + 1)
                            for j in range(4):
                                last = nc.tensor.transpose(bank[e][:, j * P:(j + 1) * P], xn[:, e, j, :], ident)
                            last.then_inc(s_tr, 1)

        wo_sb = sb("wo_sb", [P, HEADS // 2, D])
        tab = sb("tab", [P, 4, BT, DH])
        scales = sb("scales", [P, 4, DEPTH, DH])
        par_all = sb("par_all", [P, DEPTH, B_ALL])

        def load_att_weights(sp, stage, layer):
            sp.dma_start(stage[:, :], wqkv[ds(layer, 1), :, :].rearrange("l p n -> (l p) n")).then_inc(w_att, 16)
            sp.dma_start(wo_sb[:, :, :], wo[ds(layer, 1), :, :].rearrange("l (c p) n -> (l p) c n", p=P)).then_inc(w_att, 16)

        def make_tables(pool, layer, count):
            for k in range(4):
                nc.gpsimd.tensor_tensor(tab[:, k, :, :], rot[:, k, :, :],
                                        scales[:, k, ds(layer, 1), :].broadcast_to([P, BT, DH]),
                                        ALU.mult).then_inc(count, 1)

        att_out = nc.dram_tensor("att_out", [TOK, D], fp32).ap()
        with ExitStack() as scope:
            aw = sb("aw", [P, 3 * D], scope=scope)
            awout = sb("awout", [P, D], scope=scope)
            ab = sb("ab", [P, 3], scope=scope)
            about = sb("about", [P, D], scope=scope)
            xh = sb("xh", [P, TILES, D], scope=scope)
            kT = sb("kT_a", [P, TOK], scope=scope)
            vt = sb("vt_a", [P, TILES, D], scope=scope)
            vTc = sb("vTc", [P, 2, CHUNK], scope=scope)
            xl = sb("xl", [P, BATCH, NM], scope=scope)
            ql, kl = sb("ql", [P, BATCH, NM], scope=scope), sb("kl", [P, BATCH, NM], scope=scope)
            qlb = sb("qlb", [P, BATCH, NH, NM], scope=scope)
            klb = sb("klb", [P, BATCH, NH, NM], scope=scope)
            zb = sb("zb", [P, BATCH * PAIRS, 2 * NDH], scope=scope)
            yb = sb("yb", [P, BATCH * PAIRS, 2 * NDH], scope=scope)
            qscale = 1.0 / math.sqrt(NDH)
            a_in, a_bias, a_land, a_lp, a_ql = (sem(n) for n in ("a_in", "a_bias", "a_land", "a_lp", "a_ql"))

            with nc.Block() as block:
                @block.sync
                def _(sp):
                    sp.dma_start(aw[:, :], a_wqkv).then_inc(a_in, 16)
                    with nc.allow_non_contiguous_dma(reason="a few per-feature parameters"):
                        sp.dma_start(ab[:, :], a_bqkv.rearrange("(k p) -> p k", p=P)).then_inc(a_in, 16)
                    sp.dma_start(awout[:, :], a_wout).then_inc(a_in, 16)
                    sp.dma_start(about[:, :], a_bout.partition_broadcast(P)).then_inc(a_in, 16)
                    sp.dma_start(xh[:, :, :], hid.rearrange("b (n p) d -> p (b n) d", p=P)).then_inc(a_in, 16)
                    loads = []
                    for k, src in ((0, q_scale), (2, k_scale)):
                        loads.append((scales[:, k, :, :], src.partition_broadcast(P)))
                        for h in range(2):
                            loads.append((scales[:, k + 1, :, h * HALF:(h + 1) * HALF],
                                          src[:, (1 - h) * HALF:(2 - h) * HALF].partition_broadcast(P)))
                    for k in range(FK):
                        for at, off in ((B_VAL, 0), (B_GATE, FF)):
                            loads.append((par_all[0:FROWS[k], :, at + k],
                                          b1[:, off + k * P:off + k * P + FROWS[k]].rearrange("l p -> p l")))
                    for at, src in ((B_G, ln_g), (B_B, ln_b), (B_B2, b2)):
                        loads.append((par_all[:, :, at], src.rearrange("l p -> p l")))
                    sp.wait_ge(f_par, 1)
                    with nc.allow_non_contiguous_dma(reason="a few per-feature parameters"):
                        for dst, src in loads:
                            sp.dma_start(dst, src).then_inc(loaded, 16)
                    sp.wait_ge(a_in, 80)

                @block.gpsimd
                def _(pool):
                    nc.gpsimd.memset(par_all[:, :, :], 0.0).then_inc(f_par, 1)
                    pool.wait_ge(a_in, 80)
                    nc.gpsimd.tensor_tensor(xh[:, :, :], xh[:, :, :], about[:, :].unsqueeze(1).broadcast_to([P, TILES, D]),
                                            ALU.add).then_inc(a_bias, 1)

                @block.vector
                def _(dve):
                    for b in range(BATCH):
                        nc.vector.tensor_reduce(xl[:, b, :], xa[:, b * XCOLS + 1:(b + 1) * XCOLS].rearrange("p (m l) -> p m l", l=NL),
                                                AX.X, ALU.add).then_inc(a_land, 1)
                    dve.wait_ge(a_in, 80)
                    nc.vector.tensor_scalar(ab[:, 0:1], ab[:, 0:1], qscale, None, ALU.mult).then_inc(a_bias, 1)
                    dve.wait_ge(a_bias, 2)
                    dve.wait_ge(a_lp, 2)
                    nc.vector.tensor_scalar(ql[:, :, :], bank[0][:, 0:BATCH * NM].rearrange("p (b m) -> p b m", b=BATCH), qscale / NL, ab[:, 0:1],
                                            ALU.mult, ALU.add).then_inc(a_ql, 1)
                    nc.vector.tensor_scalar(kl[:, :, :], bank[1][:, 0:BATCH * NM].rearrange("p (b m) -> p b m", b=BATCH), 1.0 / NL, ab[:, 1:2],
                                            ALU.mult, ALU.add).then_inc(a_ql, 1)
                    dve.wait_ge(a_ql, 2)
                    heads = consts[:, C_HEAD:C_HEAD + NH].unsqueeze(2).broadcast_to([P, NH, NM])
                    for b in range(BATCH):
                        for src, dst in ((ql, qlb), (kl, klb)):
                            nc.vector.tensor_tensor(dst[:, b, :, :], src[:, b, :].unsqueeze(1).broadcast_to([P, NH, NM]),
                                                    heads, ALU.mult).then_inc(a_ql, 1)

                @block.scalar
                def _(act):
                    def step(at):
                        u = at(0)
                        if u:
                            act.wait_ge(a_k_mm, upto(u.g))
                            nc.scalar.activation(kT[:, ds(u.tile * CHUNK, CHUNK)], bank[2 + u.slot][:, :], ACT.Identity,
                                                 bias=ab[:, 1:2]).then_inc(a_kT, 1)
                            act.wait_ge(a_v_mm, upto(u.g))
                            act.wait_ge(a_vtr, upto(u.g - 2))
                            nc.scalar.activation(vTc[:, u.slot, :], bank[4 + u.slot][:, :], ACT.Identity,
                                                 bias=ab[:, 2:3]).then_inc(a_vT, 1)
                        u = at(1)
                        if u:
                            act.wait_ge(a_vtr, upto(u.g))
                            nc.scalar.copy(vt[:, ds(u.tile * 4, 4), :], bank[6 + u.slot][:, :].rearrange("p (a c) -> p a c", a=4))\
                                .then_inc(a_v, 1)
                    run_steps(act, 0, step, CHUNKS, 2, 2, 1)

                @block.tensor
                def _(pe):
                    pe.wait_ge(a_in, 80)
                    pe.wait_ge(a_land, 2)
                    for k in range(2):
                        nc.tensor.matmul(bank[k][:, 0:BATCH * NM], aw[:, k * D:(k + 1) * D], xl[:, :, :].rearrange("p b m -> p (b m)"),
                                         start=True, stop=True).then_inc(a_lp, 1)

                    def step(at):
                        u = at(0)
                        if u:
                            x = xa[:, ds(u.tile * CHUNK + u.tile // (CHUNKS // BATCH) + 1, CHUNK)]
                            pe.wait_ge(a_kT, upto(u.g - 2))
                            nc.tensor.matmul(bank[2 + u.slot][:, :], aw[:, D:2 * D], x, start=True, stop=True).then_inc(a_k_mm, 1)
                            pe.wait_ge(a_vT, upto(u.g - 2))
                            nc.tensor.matmul(bank[4 + u.slot][:, :], aw[:, 2 * D:3 * D], x, start=True, stop=True).then_inc(a_v_mm, 1)
                        u = at(1)
                        if u:
                            pe.wait_ge(a_vT, upto(u.g))
                            pe.wait_ge(a_v, upto(u.g - 2))
                            for j in range(4):
                                last = nc.tensor.transpose(bank[6 + u.slot][:, j * P:(j + 1) * P], vTc[:, u.slot, j * P:(j + 1) * P], ident)
                            last.then_inc(a_vtr, 1)
                    run_steps(pe, 0, step, CHUNKS, 2, 2, 1)

            with ExitStack() as inner:
                qb = sb("qb_a", [P, 2, P], scope=inner)
                p3 = sb("p3", [P, 2, SEQ], scope=inner)
                p3T = sb("p3T", [P, 2, CHUNK], scope=inner)
                nmx = sb("nmx", [P, 2], scope=inner)
                sum3, rsum3 = sb("sum3", [P, 2], scope=inner), sb("rsum3", [P, 2], scope=inner)
                s3 = psum[:, 0:SEQ]
                with nc.Block() as block:
                    def copy_transposed(eng, copy, g, j):
                        eng.wait_ge(b_tr, QLEAD + 4 * g + j + 1)
                        eng.wait_ge(b_u, QLEAD + 4 * g + j - 1)
                        copy(p3T[:, j % 2, :], bank[4 + j % 2][:, :]).then_inc(b_pT[j // 2], 1)

                    @block.gpsimd
                    def _(pool):
                        def step(at):
                            u = at(0)
                            if u:
                                pool.wait_ge(b_s, upto(u.g - 2))
                                nc.gpsimd.tensor_copy(qb[:, u.slot, :], qlb[:, :, :, :].rearrange("p b h m -> p (b h m)")[:, ds(u.tile * P, P)])\
                                    .then_inc(b_q, 1)
                        run_steps(pool, 0, step, BATCH * PAIRS, 2, 2, 1)

                    @block.vector
                    def _(dve):
                        def step(at):
                            u = at(0)
                            if u:
                                dve.wait_ge(b_s, upto(u.g))
                                dve.wait_ge(b_e, upto(u.g - 2))
                                nc.vector.tensor_reduce(nmx[:, u.slot:u.slot + 1], s3, AX.X, ALU.max, negate=True).then_inc(b_max, 1)
                            u = at(1)
                            if u:
                                for j in (2, 3):
                                    copy_transposed(dve, nc.vector.tensor_copy, u.g, j)
                            u = at(0)
                            if u:
                                dve.wait_ge(b_e, upto(u.g))
                                dve.wait_ge(b_z, upto(u.g - 2))
                                nc.vector.reciprocal(rsum3[:, u.slot:u.slot + 1], sum3[:, u.slot:u.slot + 1]).then_inc(b_rs, 1)
                            u = at(1)
                            if u:
                                dve.wait_ge(b_rs, upto(u.g))
                                dve.wait_ge(b_u, QLEAD + 4 * u.g + 4)
                                nc.vector.scalar_tensor_tensor(
                                    out=zb[:, ds(u.tile, 1), :].rearrange("p a b -> p (a b)"),
                                    in0=bank[6][:, ds((u.tile % PAIRS) * 2 * NDH, 2 * NDH)],
                                    scalar=rsum3[:, u.slot:u.slot + 1], in1=consts[:, C_PAIR:C_ALL], op0=ALU.mult,
                                    op1=ALU.mult).then_inc(b_z, 1)
                        run_steps(dve, 0, step, BATCH * PAIRS, 2, 2, 1)

                    @block.scalar
                    def _(act):
                        nc.scalar.preload_act_table_set("natural_log_exp_and_others")

                        def step(at):
                            u = at(1)
                            if u:
                                for j in (0, 1):
                                    copy_transposed(act, nc.scalar.copy, u.g, j)
                            u = at(0)
                            if u:
                                act.wait_ge(b_max, upto(u.g))
                                act.wait_ge(b_tr, QLEAD + 4 * (u.g - 2) + 4)
                                act.wait_ge(b_rs, upto(u.g - 2))
                                nc.scalar.activation(p3[:, u.slot, :], s3, ACT.Exp, bias=nmx[:, u.slot:u.slot + 1],
                                                     accum_out=sum3[:, u.slot:u.slot + 1]).then_inc(b_e, 1)
                        run_steps(act, 0, step, BATCH * PAIRS, 2, 2, 1)

                    @block.tensor
                    def _(pe):
                        def step(at):
                            u = at(0)
                            if u:
                                pe.wait_ge(b_q, upto(u.g))
                                pe.wait_ge(b_e, upto(u.g - 1))
                                for c in range(SEQ // CHUNK):
                                    last = nc.tensor.matmul(bank[c][:, :], qb[:, u.slot, :],
                                                            kT[:, ds((u.tile // PAIRS) * SEQ + c * CHUNK, CHUNK)], start=True, stop=True)
                                last.then_inc(b_s, 1)
                            u = at(1)
                            if u:
                                pe.wait_ge(b_z, upto(u.g - 1))
                                copied = QLEAD // 2 + 2 * u.g

                                def transposes(j):
                                    pe.wait_ge(b_pT[(j // 2 + 1) % 2], copied + j % 2 + 1 - (2 if j < 2 else 0))
                                    for i in range(4):
                                        last = nc.tensor.transpose(bank[4 + j % 2][:, i * P:(i + 1) * P],
                                                                   p3[:, u.slot, (4 * j + i) * P:(4 * j + i + 1) * P], ident)
                                    last.then_inc(b_tr, 1)

                                def products(j):
                                    pe.wait_ge(b_pT[j // 2], copied + j % 2 + 1)
                                    for i in range(4):
                                        n = 4 * j + i
                                        last = nc.tensor.matmul(
                                            bank[6][:, 0:D], p3T[:, j % 2, i * P:(i + 1) * P],
                                            vt[:, ds((u.tile // PAIRS) * BT + n, 1), :].rearrange("p a b -> p (a b)"),
                                            start=(n == 0), stop=(n == BT - 1))
                                    last.then_inc(b_u, 1)

                                transposes(0)
                                transposes(1)
                                products(0)
                                transposes(2)
                                products(1)
                                transposes(3)
                                products(2)
                                products(3)
                        run_steps(pe, 0, step, BATCH * PAIRS, 2, 2, 1)

            with ExitStack() as inner:
                GR = 4
                mats = {n: sb(n, [P, GR, GR, P], scope=inner) for n in ("x2", "x2T", "vi", "viT", "kvT", "ti")}
                x2, x2T, vi, viT, kvT, ti = mats.values()
                e2 = sb("e2", [P, BATCH * PAIRS, NM], scope=inner)
                m2, d2 = sb("m2", [P, BATCH * PAIRS], scope=inner), sb("d2", [P, BATCH * PAIRS], scope=inner)
                idc = sb("idc", [P, 3, P], scope=inner)
                c_s, c_x, c_xT = sem("c_s"), sem("c_x"), sem("c_xT")
                i_v, i_kv, i_kvT, i_t1, i_a, i_t2, i_b, i_t3, i_vn = (
                    sem(n) for n in ("i_v", "i_kv", "i_kvT", "i_t1", "i_a", "i_t2", "i_b", "i_t3", "i_vn"))
                y_mm_a, y_rd = sem("y_mm_a"), sem("y_rd")
                with nc.Block() as block:
                    @block.tensor
                    def _(pe):
                        for n in range(BATCH * PAIRS):
                            b, c = n // PAIRS, n % PAIRS
                            last = nc.tensor.matmul(bank[b][:, c * NM:(c + 1) * NM], qlb[:, b, 2 * c:2 * c + 2, :].rearrange("p h m -> p (h m)"),
                                                    kl[:, b, :], start=True, stop=True)
                        last.then_inc(c_s, 1)
                        pe.wait_ge(c_x, 9)
                        for g in range(GR):
                            for j in range(GR):
                                last = nc.tensor.transpose(bank[2 + g][:, j * P:(j + 1) * P], x2[:, g, j, :], ident)
                            last.then_inc(c_xT, 1)

                    @block.gpsimd
                    def _(pool):
                        nc.gpsimd.memset(x2[:, :, :, :], 0.0)
                        for k, v in enumerate((7.0, 15.0, 13.0)):
                            last = nc.gpsimd.tensor_scalar(idc[:, k, :], ident, v, None, ALU.mult)
                        last.then_inc(c_x, 1)
                        pool.sem_inc(i_vn, GR)
                        pool.wait_ge(loaded, 16 + 16 * 15)
                        make_tables(pool, 0, f_tab)

                    @block.vector
                    def _(dve):
                        s2 = psum[:, 0:BATCH * PAIRS * NM].rearrange("p (n m) -> p n m", m=NM)
                        dve.wait_ge(c_s, 1)
                        nc.vector.tensor_reduce(m2[:, :], s2, AX.X, ALU.max).then_inc(c_x, 1)
                        dve.wait_ge(c_x, 2)
                        nc.vector.tensor_tensor(e2[:, :, :], s2, m2[:, :].unsqueeze(2).broadcast_to([P, BATCH * PAIRS, NM]),
                                                ALU.subtract).then_inc(c_x, 1)
                        dve.wait_ge(c_x, 4)
                        nc.vector.tensor_reduce(d2[:, :], e2[:, :, :], AX.X, ALU.add).then_inc(c_x, 1)
                        dve.wait_ge(c_x, 5)
                        nc.vector.reciprocal(m2[:, :], d2[:, :]).then_inc(c_x, 1)
                        dve.wait_ge(c_x, 6)
                        x2f = x2[:, :, :, :].rearrange("p g j c -> p (g j) c")
                        for h in range(2):
                            rows = slice(64 * h, 64 * h + 64)
                            nc.vector.tensor_tensor(x2f[rows, :, 64 * h:64 * h + 64], e2[rows, :, :],
                                                    m2[rows, :].unsqueeze(2).broadcast_to([64, BATCH * PAIRS, NM]),
                                                    ALU.mult).then_inc(c_x, 1)
                        dve.wait_ge(c_x, 8)
                        nc.vector.tensor_copy(vi[:, :, :, :], x2[:, :, :, :]).then_inc(c_x, 1)

                    @block.scalar
                    def _(act):
                        act.wait_ge(c_x, 3)
                        nc.scalar.activation(e2[:, :, :], e2[:, :, :], ACT.Exp).then_inc(c_x, 1)
                        for g in range(GR):
                            act.wait_ge(c_xT, g + 1)
                            src = bank[2 + g][:, :].rearrange("p (j c) -> p j c", j=GR)
                            nc.scalar.copy(x2T[:, g, :, :], src)
                            nc.scalar.copy(viT[:, g, :, :], src).then_inc(i_v, 1)

                with nc.Block() as block:
                    def product(out_bank, left_T, right, g, count):
                        for j in range(GR):
                            last = nc.tensor.matmul(out_bank[:, j * P:(j + 1) * P], left_T[:, g, j, :], right[:, g, j, :],
                                                    start=True, stop=True)
                        if count is not None:
                            last.then_inc(count, 1)

                    @block.tensor
                    def _(pe):
                        with pe.Fori(0, PINV_ITERS) as it:
                            n = pe.snap(GR * it)
                            for g in range(GR):
                                pe.wait_ge(i_v, n + g + 1)
                                product(bank[2 * g], x2T, vi, g, None)
                                product(bank[2 * g + 1], vi, x2T, g, i_kv)
                            for g in range(GR):
                                pe.wait_ge(i_kvT, n + g + 1)
                                pe.wait_ge(i_t1, n + g + 1)
                                product(bank[2 * g], kvT, ti, g, i_a)
                            for g in range(GR):
                                pe.wait_ge(i_t2, n + g + 1)
                                product(bank[2 * g], kvT, ti, g, i_b)
                            for g in range(GR):
                                pe.wait_ge(i_t3, n + g + 1)
                                product(bank[2 * g], viT, ti, g, None)
                                product(bank[2 * g + 1], ti, viT, g, i_vn)
                        pe.wait_ge(i_v, GR * PINV_ITERS + GR)
                        for m in range(BATCH * PAIRS):
                            last = nc.tensor.matmul(bank[0][:, m * 2 * NDH:(m + 1) * 2 * NDH], viT[:, m // GR, m % GR, :],
                                                    zb[:, m, :], start=True, stop=True)
                        last.then_inc(y_mm_a, 1)

                    @block.vector
                    def _(dve):
                        with dve.Fori(0, PINV_ITERS) as it:
                            n = dve.snap(GR * it)
                            for k, (ready, done) in enumerate(((i_kv, i_t1), (i_a, i_t2), (i_b, i_t3))):
                                for g in range(GR):
                                    dve.wait_ge(ready, n + g + 1)
                                    if k == 0:
                                        dve.wait_ge(i_vn, n + g + 1)
                                    nc.vector.tensor_tensor(ti[:, g, :, :], idc[:, k, :].unsqueeze(1).broadcast_to([P, GR, P]),
                                                            bank[2 * g][:, :].rearrange("p (j c) -> p j c", j=GR),
                                                            ALU.subtract).then_inc(done, 1)
                        dve.wait_ge(y_mm_a, 1)
                        nc.vector.tensor_copy(yb[:, :, :], bank[0][:, 0:BATCH * PAIRS * 2 * NDH].rearrange("p (n c) -> p n c", c=2 * NDH))\
                            .then_inc(y_rd, 1)

                    @block.scalar
                    def _(act):
                        with act.Fori(0, PINV_ITERS) as it:
                            n = act.snap(GR * it)
                            for g in range(GR):
                                act.wait_ge(i_kv, n + g + 1)
                                nc.scalar.copy(kvT[:, g, :, :], bank[2 * g + 1][:, :].rearrange("p (j c) -> p j c", j=GR)).then_inc(i_kvT, 1)
                            for g in range(GR):
                                act.wait_ge(i_vn, n + GR + g + 1)
                                nc.scalar.mul(vi[:, g, :, :], bank[2 * g][:, :].rearrange("p (j c) -> p j c", j=GR), 0.25)
                                nc.scalar.mul(viT[:, g, :, :], bank[2 * g + 1][:, :].rearrange("p (j c) -> p j c", j=GR), 0.25).then_inc(i_v, 1)

            with ExitStack() as inner:
                yp = sb("yp", [P, BATCH, PAIRS * (P + 2 * NDH)], scope=inner)
                qTa = sb("qTa", [P, 2, P], scope=inner)
                sub1 = sb("sub1", [P, NH, NM], scope=inner)
                m1, d1, rd1 = sb("m1", [P, NH], scope=inner), sb("d1", [P, NH], scope=inner), sb("rd1", [P, 2, NH], scope=inner)
                p1 = sb("p1", [P, 2, NH, NM], scope=inner)
                p1T = sb("p1T", [P, 2, PAIRS, P], scope=inner)
                oTa = sb("oTa", [P, 2, P], scope=inner)
                s1 = psum[:, 512:512 + NH * NM].rearrange("p (h m) -> p h m", m=NM)
                d_yp = sem("d_yp")
                STORE = 4
                a_store = sem("a_store")
                with nc.Block() as block:
                    @block.gpsimd
                    def _(pool):
                        nc.gpsimd.memset(yp[:, :, :], 0.0).then_inc(d_yp, 1)
                        pool.wait_ge(d_yp, 1)
                        for b in range(BATCH):
                            nc.gpsimd.tensor_copy(yp[:, b, :].rearrange("p (n c) -> p n c", n=PAIRS)[:, :, 0:2 * NDH],
                                                  yb[:, b * PAIRS:(b + 1) * PAIRS, :]).then_inc(d_yp, 1)

                        def step(at):
                            u = at(1)
                            if u:
                                pool.wait_ge(d_rd, upto(u.g))
                                nc.gpsimd.tensor_tensor(p1[:, u.slot, :, :], p1[:, u.slot, :, :],
                                                        rd1[:, u.slot, :].unsqueeze(2).broadcast_to([P, NH, NM]), ALU.mult).then_inc(d_n, 1)
                        run_steps(pool, 0, step, TILES, 4, 2, 1)

                    @block.sync
                    def _(sp):
                        dst = att_out.rearrange("(n p) d -> p n d", p=P)
                        for n in range(0, BT, STORE):
                            sp.wait_ge(d_add, LEAD + BATCH * (n + STORE))
                            for b in range(BATCH):
                                tiles = slice(b * BT + n, b * BT + n + STORE)
                                sp.dma_start(dst[:, tiles, :], xh[:, tiles, :]).then_inc(a_store, 16)
                        sp.wait_ge(a_store, 16 * BATCH * (BT // STORE))

                    @block.scalar
                    def _(act):
                        def step(at):
                            u = at(0)
                            if u:
                                act.wait_ge(d_q, upto(u.g))
                                act.wait_ge(d_s, upto(u.g - 2))
                                nc.scalar.activation(qTa[:, u.slot, :], bank[0][:, 0:P], ACT.Identity, scale=qscale, bias=ab[:, 0:1])\
                                    .then_inc(d_qT, 1)
                            u = at(3)
                            if u:
                                act.wait_ge(d_tr, upto(u.g))
                                act.wait_ge(d_o, upto(u.g - 2))
                                nc.scalar.copy(p1T[:, u.slot, :, :], psum[:, 3 * 512:5 * 512].rearrange("p (n c) -> p n c", n=PAIRS)).then_inc(d_pT, 1)
                            u = at(1)
                            if u:
                                act.wait_ge(d_sub, upto(u.g))
                                act.wait_ge(d_tr, upto(u.g - 2))
                                nc.scalar.activation(p1[:, u.slot, :, :], sub1[:, :, :], ACT.Exp).then_inc(d_e, 1)
                            u = at(3)
                            if u:
                                act.wait_ge(d_o, upto(u.g))
                                act.wait_ge(d_y, upto(u.g - 2))
                                nc.scalar.copy(oTa[:, u.slot, :], bank[5][:, 0:P]).then_inc(d_oT, 1)
                        run_steps(act, 0, step, TILES, 4, 2, 1)

                    @block.vector
                    def _(dve):
                        def step(at):
                            u = at(4)
                            if u:
                                dve.wait_ge(d_y, upto(u.g))
                                a = xh[:, ds(u.slot * BT + u.tile // BATCH, 1), :].rearrange("p a b -> p (a b)")
                                nc.vector.tensor_tensor(a, bank[6][:, 0:D], a, ALU.add).then_inc(d_add, 1)
                            u = at(0)
                            if u:
                                dve.wait_ge(d_s, upto(u.g))
                                dve.wait_ge(d_sub, upto(u.g - 1))
                                nc.vector.tensor_reduce(m1[:, :], s1, AX.X, ALU.max).then_inc(d_max, 1)
                                dve.wait_ge(d_max, upto(u.g))
                                dve.wait_ge(d_e, upto(u.g - 1))
                                nc.vector.tensor_tensor(sub1[:, :, :], s1, m1[:, :].unsqueeze(2).broadcast_to([P, NH, NM]), ALU.subtract)\
                                    .then_inc(d_sub, 1)
                            u = at(1)
                            if u:
                                dve.wait_ge(d_e, upto(u.g))
                                dve.wait_ge(d_rd, upto(u.g - 1))
                                nc.vector.tensor_reduce(d1[:, :], p1[:, u.slot, :, :], AX.X, ALU.add).then_inc(d_sum, 1)
                                dve.wait_ge(d_sum, upto(u.g))
                                dve.wait_ge(d_n, upto(u.g - 2))
                                nc.vector.reciprocal(rd1[:, u.slot, :], d1[:, :]).then_inc(d_rd, 1)
                        run_steps(dve, 0, step, TILES, 4, 2, 1)

                    @block.tensor
                    def _(pe):
                        def step(at):
                            u = at(0)
                            if u:
                                pe.wait_ge(d_qT, upto(u.g - 1))
                                nc.tensor.matmul(bank[0][:, 0:P], aw[:, 0:D], xa[:, ds(u.slot * XCOLS + 1 + (u.tile // BATCH) * P, P)], start=True, stop=True)\
                                    .then_inc(d_q, 1)
                            u = at(3)
                            if u:
                                pe.wait_ge(d_n, upto(u.g))
                                pe.wait_ge(d_pT, upto(u.g - 1))
                                for c in range(PAIRS):
                                    last = nc.tensor.transpose(psum[:, 3 * 512 + c * P:3 * 512 + (c + 1) * P],
                                                               p1[:, u.slot, 2 * c:2 * c + 2, :].rearrange("p h m -> p (h m)"), ident)
                                last.then_inc(d_tr, 1)
                            u = at(4)
                            if u:
                                pe.wait_ge(d_oT, upto(u.g))
                                pe.wait_ge(d_add, upto(u.g - 1))
                                nc.tensor.matmul(bank[6][:, 0:D], oTa[:, u.slot, :], awout[:, :], start=True, stop=True).then_inc(d_y, 1)
                            u = at(0)
                            if u:
                                pe.wait_ge(d_qT, upto(u.g))
                                pe.wait_ge(d_sub, upto(u.g - 1))
                                for c in range(2):
                                    last = nc.tensor.matmul(bank[1 + c][:, :], qTa[:, u.slot, :],
                                                            klb[:, u.slot, c * 8:(c + 1) * 8, :].rearrange("p h m -> p (h m)"),
                                                            start=True, stop=True)
                                last.then_inc(d_s, 1)
                            u = at(3)
                            if u:
                                pe.wait_ge(d_yp, 1 + BATCH)
                                pe.wait_ge(d_pT, upto(u.g))
                                pe.wait_ge(d_oT, upto(u.g - 1))
                                for c in range(PAIRS):
                                    last = nc.tensor.matmul(bank[5][:, 0:P], yp[:, u.slot, c * P:(c + 1) * P], p1T[:, u.slot, c, :],
                                                            start=(c == 0), stop=(c == PAIRS - 1))
                                last.then_inc(d_o, 1)
                        run_steps(pe, 0, step, TILES, 4, 2, 1)

        w1_sb = sb("w1_sb", [P, 2 * FF])
        w2_sb = sb("w2_sb", [P, FK, D])
        par = sb("par", [P, B_ALL])
        xt = sb("xt", [P, TILES, D])
        stats = sb("stats", [P, TILES, 6])
        small = sb("small", [P, 6, TILES])
        wqkv_hi, wqkv_lo = sb("wqkv_hi", [P, 3 * INNER], part), sb("wqkv_lo", [P, 3 * INNER], part)
        vtok = sb("vtok", [P, 2, 2, 2, UP * DH])
        v2 = sb("v2", [P, 2, WINS, 2, 2, UP * DH])
        kb = sb("kb", [P, 2, UP, 2, WIN + P])

        with ExitStack() as scope:
            stage = sb("stage0", [P, 3 * INNER], scope=scope)
            with nc.Block() as block:
                @block.sync
                def _(sp):
                    load_att_weights(sp, stage, 0)
                    sp.wait_ge(w_att, 32)

                @block.scalar
                def _(act):
                    act.wait_ge(w_att, 32)
                    nc.scalar.copy(wqkv_hi[:, :], stage[:, :]).then_inc(w_split, 1)

                @block.vector
                def _(dve):
                    nc.vector.memset(v2[:, :, :, :, :, :], 0.0)
                    dve.wait_ge(w_att, 32)
                    dve.wait_ge(w_split, 1)
                    nc.vector.tensor_tensor(wqkv_lo[:, :], stage[:, :], wqkv_hi[:, :], ALU.subtract)

                @block.gpsimd
                def _(pool):
                    nc.gpsimd.memset(kb[:, :, :, :, :], 0.0)
                    nc.gpsimd.memset(vtok[:, :, :, :, :], 0.0)

        with nc.Fori(0, DEPTH) as layer:
            with ExitStack() as scope:
                xs = sb("xs", [P, P], scope=scope)
                xs_hi, xs_lo = sb("xs_hi", [P, P], part, scope=scope), sb("xs_lo", [P, P], part, scope=scope)
                xf = sb("xf", [P, P], scope=scope)
                raw = sb("raw", [P, 2, 2, UH, DH], scope=scope)
                sq = sb("sq", [P, 2 * UW], scope=scope)
                ss0, ss = sb("ss0", [P, 2 * UH], scope=scope), sb("ss", [P, 2, 2 * UH], scope=scope)
                lns, r0 = sb("lns", [P, 2 * UH], scope=scope), sb("r0", [P, 2, 2 * UH], scope=scope)
                r1, r = sb("r1", [P, 2 * UH], scope=scope), sb("r", [P, 2, 2 * UH], scope=scope)
                rc = sb("rc", [P, 2, UH, DH], scope=scope)
                rs = sb("rs", [P, 2, UH, DH], scope=scope)
                qkn = sb("qkn", [P, 2, UH, DH], scope=scope)
                qT = sb("qT", [P, UP, P], scope=scope)
                sm = sb("sm", [P, 2, UH], scope=scope)
                sub = sb("sub", [P, UH, 2 * WIN], scope=scope)
                e = sb("e", [P, 2, UH, 2 * WIN], scope=scope)
                den, rden = sb("den", [P, UH], scope=scope), sb("rden", [P, 2, UH], scope=scope)
                pT = sb("pT", [P, 2, UP, P], scope=scope)
                o = sb("o", [P, UH, DH], scope=scope)
                oT = sb("oT", [P, 2, UP, P], scope=scope)
                bA, bT, bS, bO, bX, bY = bank[0:2], bank[2:4], bank[4], bank[5], bank[6], bank[7]
                with nc.Block() as block:
                    @block.sync
                    def _(sp):
                        sp.dma_start(w1_sb[:, :], w1[ds(layer, 1), :, :].rearrange("l p n -> (l p) n")).then_inc(w_ffn, 16)
                        sp.dma_start(w2_sb[:, 0:2, :], w2[ds(layer, 1), 0:2 * P, :].rearrange(
                            "l (c p) n -> (l p) c n", p=P)).then_inc(w_ffn, 16)
                        sp.dma_start(w2_sb[0:FROWS[2], 2, :], w2[ds(layer, 1), 2 * P:FF, :].rearrange(
                            "l p n -> (l p) n")).then_inc(w_ffn, 16)

                        def step(at):
                            u = at(0)
                            if u and u.half == 1:
                                sp.wait_ge(v_raw, upto(u.g))
                                for hp in range(2):
                                    rows = hp * 64
                                    sp.dma_start(v2[rows:rows + WIN, u.slot, 0, hp, :, :], vtok[P - WIN:P, 1 - u.slot, hp, :, :])\
                                        .then_inc(v2_tail, 16)
                                for hp in range(2):
                                    rows = hp * 64
                                    tok, by_win = vtok[:, u.slot, hp, :, :], v2[:, u.slot, :, hp, :, :]
                                    sp.dma_start(by_win[rows + WIN:rows + 2 * WIN, 0, :, :], tok[0:WIN, :, :])\
                                        .then_inc(v2_ready[u.slot], 16)
                                    for w in range(1, WINS):
                                        sp.dma_start(by_win[rows:rows + 2 * WIN, w, :, :], tok[(w - 1) * WIN:(w + 1) * WIN, :, :])\
                                            .then_inc(v2_ready[u.slot], 16)
                        run_steps(sp, layer, step, UNITS, ATT_LAG, 4, 2)

                    @block.gpsimd
                    def _(pool):
                        def step(at):
                            u = at(0)
                            if u and u.half == 0:
                                pool.wait_ge(v_mm, upto(u.g - 1))
                                pool.wait_ge(sin_done, upto(u.g - 1))
                                pool.sem_inc(xs_begun, 1)
                                nc.gpsimd.tensor_copy(xs[0:64, :], xa[0:64, ds(col(u.tile), P)]).then_inc(xs_ready, 1)
                                nc.gpsimd.tensor_copy(xs[64:P, :], xa[64:P, ds(col(u.tile) - 1, P)]).then_inc(xs_ready, 1)
                                pool.wait_ge(xs_ready, upto(u.g) + 1)
                                pool.sem_inc(xs_begun, 1)
                                nc.gpsimd.tensor_copy(xs_hi[:, :], xs[:, :]).then_inc(xs_high, 1)
                                pool.wait_ge(xs_high, upto(u.tg))
                                nc.gpsimd.tensor_tensor(xs_lo[:, :], xs[:, :], xs_hi[:, :], ALU.subtract).then_inc(xs_low, 1)
                            u = at(6)
                            if u and u.half == 1:
                                pool.wait_ge(y_used, upto(u.tg))
                                pool.wait_ge(f1_mm, upto(u.tg - 1))
                                if at(1):
                                    pool.wait_ge(sin_done, upto(at(1).g))
                                elif at(2):
                                    pool.wait_ge(kn_ready, upto(at(2).g))
                                pool.sem_inc(xf_begun, 1)
                                nc.gpsimd.tensor_copy(xf[0:64, :], xa[0:64, ds(col(u.tile), P)]).then_inc(f1_low, 1)
                                nc.gpsimd.tensor_copy(xf[64:P, :], xa[64:P, ds(col(u.tile) - 1, P)]).then_inc(f1_x, 1)
                                pool.wait_ge(f1_x, upto(u.tg))
                            u = at(1)
                            if u:
                                h = u.half
                                pool.wait_ge(r_ready, upto(u.g))
                                pool.wait_ge(rot_ready, upto(u.g))
                                pool.wait_ge(kT_mm, upto(u.g - 1))
                                for k, done in enumerate((qn_ready, kn_ready)):
                                    nc.gpsimd.tensor_tensor(qkn[:, k, :, :], rc[:, k, :, :],
                                                            r[:, h, k * UH:(k + 1) * UH].unsqueeze(2).broadcast_to([P, UH, DH]),
                                                            ALU.mult).then_inc(done, 1)
                            u = at(0)
                            if u:
                                h = u.half
                                pool.wait_ge(f_tab, 4)
                                pool.wait_ge(q_raw, upto(u.g))
                                pool.wait_ge(k_raw, upto(u.g))
                                pool.wait_ge(rot_ready, upto(u.g - 1))
                                tt = pool.snap(u.tile % BT) if not isinstance(u.tile, int) else u.tile % BT
                                for hf in range(2):
                                    last = nc.gpsimd.tensor_tensor(
                                        rs[:, :, :, hf * HALF:(hf + 1) * HALF],
                                        raw[:, h, :, :, (1 - hf) * HALF:(2 - hf) * HALF],
                                        tab[:, 1::2, ds(tt, 1), hf * HALF:(hf + 1) * HALF].broadcast_to([P, 2, UH, HALF]),
                                        ALU.mult)
                                last.then_inc(sin_done, 1)
                        run_steps(pool, layer, step, UNITS, ATT_LAG, 4, 2)

                    @block.scalar
                    def _(act):
                        nc.scalar.preload_act_table_set("natural_log_exp_and_others")

                        def step(at):
                            u = at(0)
                            if u:
                                h = u.half
                                act.wait_ge(cos_done, upto(u.g - 2))
                                act.wait_ge(sin_done, upto(u.g - 2))
                                act.wait_ge(q_mm, upto(u.g))
                                nc.scalar.copy(raw[:, h, 0, :, :], bA[h][:, :].rearrange("p (h d) -> p h d", d=DH)).then_inc(q_raw, 1)
                                act.wait_ge(k_mm, upto(u.g))
                                nc.scalar.copy(raw[:, h, 1, :, :], bA[1 - h][:, :].rearrange("p (h d) -> p h d", d=DH)).then_inc(k_raw, 1)
                                act.wait_ge(ss_sum, upto(u.g - 1))
                                nc.scalar.activation(sq[:, 0:UW], bA[h][:, :], ACT.Square).then_inc(q_sq, 1)
                                nc.scalar.activation(sq[:, UW:2 * UW], bA[1 - h][:, :], ACT.Square).then_inc(k_sq, 1)
                            u = at(7)
                            if u and u.half == 1:
                                act.wait_ge(f1_mm, upto(u.tg))
                                nc.scalar.copy(xt[:, ds(u.tile, 1), :].rearrange("p a b -> p (a b)"), bY[:, P:2 * P]).then_inc(f1_tok, 1)
                            u = at(4)
                            if u:
                                act.wait_ge(oT_mm, upto(u.g))
                                act.wait_ge(y_mm, upto(u.g - 2))
                                nc.scalar.copy(oT[:, u.half, :, :], bX[:, :].rearrange("p (a c) -> p a c", a=UP))\
                                    .then_inc(oT_ready, 1)
                            u = at(1)
                            if u:
                                act.wait_ge(qT_mm, upto(u.g))
                                act.wait_ge(s_mm, upto(u.g - 1))
                                nc.scalar.copy(qT[:, :, :], bT[0][:, :].rearrange("p (a c) -> p a c", a=UP))\
                                    .then_inc(qT_ready, 1)
                            u = at(1)
                            if u:
                                act.wait_ge(halo_ready, upto(u.g))
                                act.wait_ge(kT_mm, upto(u.g))
                                for hp in range(2):
                                    rows = slice(64 * hp, 64 * hp + 64)
                                    last = nc.scalar.copy(kb[rows, u.half, :, hp, WIN:WIN + P],
                                                          bT[1][rows, :].rearrange("p (a c) -> p a c", a=UP))
                                last.then_inc(kb_ready, 1)
                            u = at(0)
                            if u:
                                h = u.half
                                act.wait_ge(v_mm, upto(u.g))
                                act.wait_ge(v2_ready[u.slot], V2_LEAD + V2_TILE * ((u.tg - u.slot) // 2))
                                act.wait_ge(v2_tail, V2_LEAD + V2_TAIL * u.tg)
                                if h == 1:
                                    act.wait_ge(av_mm, upto(u.g - 4))
                                nc.scalar.copy(vtok[:, u.slot, :, h, :], bA[h][:, :].rearrange("p (a c) -> p a c", a=2))\
                                    .then_inc(v_raw, 1)
                            u = at(0)
                            if u:
                                act.wait_ge(ss_ready, upto(u.g))
                                nc.scalar.activation(lns[:, :], ss[:, u.half, :], ACT.Ln, scale=R_SCALE ** 2)\
                                    .then_inc(ln_done, 1)
                                act.wait_ge(ln_done, upto(u.g))
                                nc.scalar.activation(r0[:, u.half, :], lns[:, :], ACT.Exp, scale=-0.5).then_inc(r0_ready, 1)
                            u = at(2)
                            if u:
                                act.wait_ge(sub_done, upto(u.g))
                                act.wait_ge(pT_mm, upto(u.g - 2))
                                act.wait_ge(den_done, upto(u.g - 2))
                                nc.scalar.activation(e[:, u.half, :, :], sub[:, :, :], ACT.Exp).then_inc(e_ready, 1)
                            u = at(0)
                            if u:
                                act.wait_ge(s_mm, upto(u.g - 2))
                                act.wait_ge(kb_ready, upto(u.g - 2))
                                for hp in range(2):
                                    rows = slice(64 * hp, 64 * hp + 64)
                                    last = nc.scalar.activation(kb[rows, u.half, :, hp, 0:WIN], kb[rows, u.half, :, hp, P:P + WIN],
                                                                ACT.Copy, scale=halo_decay[rows, :])
                                last.then_inc(halo_ready, 1)
                            u = at(2)
                            if u:
                                act.wait_ge(pT_mm, upto(u.g))
                                act.wait_ge(av_mm, upto(u.g - 2))
                                nc.scalar.copy(pT[:, u.half, :, :], bX[:, :].rearrange("p (a c) -> p a c", a=UP))\
                                    .then_inc(pT_ready, 1)
                        run_steps(act, layer, step, UNITS, ATT_LAG, 4, 2)
                        act.wait_ge(f_stat, (STATS + REFINE) * layer + STATS)
                        rsqrt_seed(act, small, f_ln, 2 * layer)

                    @block.vector
                    def _(dve):
                        def step(at):
                            s = bS[:, :].rearrange("p (h c) -> p h c", c=2 * WIN)
                            u = at(0)
                            if u:
                                h = u.half
                                dve.wait_ge(q_raw, upto(u.g))
                                dve.wait_ge(k_raw, upto(u.g))
                                dve.wait_ge(kn_ready, upto(u.g - 1))
                                tt = u.tile % BT
                                nc.vector.tensor_tensor(rc[:, :, :, :], raw[:, h, :, :, :],
                                                        tab[:, 0::2, ds(tt, 1), :].broadcast_to([P, 2, UH, DH]),
                                                        ALU.mult).then_inc(cos_done, 1)
                            u = at(0)
                            if u:
                                dve.wait_ge(k_sq, upto(u.g))
                                dve.wait_ge(q_sq, upto(u.g))
                                dve.wait_ge(ss_ready, upto(u.g - 1))
                                nc.vector.tensor_reduce(ss0[:, :], sq[:, :].rearrange("p (h d) -> p h d", d=DH), AX.X, ALU.add)\
                                    .then_inc(ss_sum, 1)
                            u = at(7)
                            if u and u.half == 1:
                                dve.wait_ge(f1_tok, upto(u.tg))
                                nc.vector.bn_stats(stats[:, ds(u.tile, 1), :].rearrange("p a b -> p (a b)"),
                                                   xt[:, ds(u.tile, 1), :].rearrange("p a b -> p (a b)")).then_inc(f1_stat, 1)
                            u = at(0)
                            if u:
                                dve.wait_ge(ss_sum, upto(u.g))
                                dve.wait_ge(nt_half, upto(u.g - 2))
                                nc.vector.tensor_scalar(ss[:, u.half, :], ss0[:, :], 1e-24, None, ALU.max).then_inc(ss_ready, 1)
                            u = at(0)
                            if u:
                                h = u.half
                                dve.wait_ge(sin_done, upto(u.g))
                                dve.wait_ge(cos_done, upto(u.g))
                                nc.vector.tensor_tensor(rc[:, :, :, :], rc[:, :, :, :], rs[:, :, :, :], ALU.add)\
                                    .then_inc(rot_ready, 1)
                            u = at(0)
                            if u:
                                h = u.half
                                dve.wait_ge(r0_ready, upto(u.g))
                                dve.wait_ge(nt_half, upto(u.g - 1))
                                dve.wait_ge(r_ready, upto(u.g - 1))
                                nc.vector.tensor_tensor(r1[:, :], r0[:, h, :], r0[:, h, :], ALU.mult).then_inc(nt_sq, 1)
                                dve.wait_ge(nt_sq, upto(u.g))
                                nc.vector.scalar_tensor_tensor(out=r1[:, :], in0=r1[:, :], scalar=-0.5 * R_SCALE ** 2,
                                                               in1=ss[:, h, :], op0=ALU.mult, op1=ALU.mult).then_inc(nt_half, 1)
                                dve.wait_ge(nt_half, upto(u.g))
                                dve.wait_ge(qn_ready, upto(u.g - 2))
                                dve.wait_ge(kn_ready, upto(u.g - 2))
                                nc.vector.scalar_tensor_tensor(out=r[:, h, :], in0=r1[:, :], scalar=1.5, in1=r0[:, h, :],
                                                               op0=ALU.add, op1=ALU.mult).then_inc(r_ready, 1)
                            u = at(4)
                            if u and u.half == 1:
                                dve.wait_ge(y_mm, upto(u.g))
                                nc.vector.tensor_tensor(xa[:, ds(col(u.tile), P)], bY[:, 0:P], xa[:, ds(col(u.tile), P)],
                                                        ALU.add).then_inc(y_used, 1)
                            u = at(3)
                            if u:
                                dve.wait_ge(av_mm, upto(u.g))
                                dve.wait_ge(rden_ready, upto(u.g))
                                dve.wait_ge(oT_mm, upto(u.g - 1))
                                nc.vector.tensor_tensor(o[:, :, :], bO[:, :].rearrange("p (h d) -> p h d", d=DH),
                                                        rden[:, u.half, :].unsqueeze(2).broadcast_to([P, UH, DH]),
                                                        ALU.mult).then_inc(o_ready, 1)
                            u = at(2)
                            if u:
                                dve.wait_ge(e_ready, upto(u.g))
                                dve.wait_ge(rden_ready, upto(u.g - 1))
                                nc.vector.tensor_reduce(den[:, :], e[:, u.half, :, :], AX.X, ALU.add).then_inc(den_done, 1)
                            u = at(1)
                            if u:
                                dve.wait_ge(s_mm, upto(u.g))
                                dve.wait_ge(sub_done, upto(u.g - 2))
                                nc.vector.tensor_reduce(sm[:, u.half, :], s, AX.X, ALU.max).then_inc(max_done, 1)
                            u = at(2)
                            if u:
                                dve.wait_ge(den_done, upto(u.g))
                                dve.wait_ge(o_ready, upto(u.g - 2))
                                nc.vector.reciprocal(rden[:, u.half, :], den[:, :]).then_inc(rden_ready, 1)
                            u = at(1)
                            if u:
                                dve.wait_ge(max_done, upto(u.g))
                                dve.wait_ge(e_ready, upto(u.g - 1))
                                nc.vector.tensor_tensor(sub[:, :, :], s, sm[:, u.half, :].unsqueeze(2).broadcast_to([P, UH, 2 * WIN]),
                                                        ALU.subtract).then_inc(sub_done, 1)
                        run_steps(dve, layer, step, UNITS, ATT_LAG, 4, 2)
                        nc.vector.tensor_copy(par[:, :], par_all[:, ds(layer, 1), :].rearrange("p a b -> p (a b)"))
                        dve.wait_ge(f1_stat, TILES * layer + TILES + LEAD)
                        finish_stats(dve, stats, small, f_stat, (STATS + REFINE) * layer)
                        dve.wait_ge(f_ln, 2 * layer + 2)
                        rsqrt_refine(dve, small, f_stat, (STATS + REFINE) * layer + STATS)

                    @block.tensor
                    def _(pe):
                        def project(out_bank, columns, done):
                            nc.tensor.matmul(out_bank, xs_hi[:, :], columns(wqkv_hi), start=True, stop=False)
                            nc.tensor.matmul(out_bank, xs_hi[:, :], columns(wqkv_lo), start=False, stop=False)
                            nc.tensor.matmul(out_bank, xs_lo[:, :], columns(wqkv_hi), start=False, stop=True).then_inc(done, 1)

                        def step(at):
                            u = at(0)
                            if u:
                                h = u.half
                                if h == 0:
                                    pe.wait_ge(w_att, 32 * layer + 32)
                                    pe.wait_ge(xs_low, upto(u.tg))
                                pe.wait_ge(k_sq, upto(u.g - 1))
                                project(bA[h][:, :], lambda w: w[:, h * UW:(h + 1) * UW], q_mm)
                                pe.wait_ge(v_raw, upto(u.g - 1))
                                project(bA[1 - h][:, :], lambda w: w[:, INNER + h * UW:INNER + (h + 1) * UW], k_mm)
                            u = at(7)
                            if u and u.half == 1:
                                pe.wait_ge(f1_x, upto(u.tg))
                                pe.wait_ge(f1_low, upto(u.tg))
                                if at(5):
                                    pe.wait_ge(y_used, upto(at(5).tg))
                                else:
                                    pe.wait_ge(f1_tok, upto(u.tg - 1))
                                nc.tensor.transpose(bY[:, P:2 * P], xf[:, :], ident).then_inc(f1_mm, 1)
                            u = at(4)
                            if u:
                                pe.wait_ge(o_ready, upto(u.g))
                                if at(3):
                                    pe.wait_ge(pT_ready, upto(at(3).g))
                                for c in range(UP):
                                    last = nc.tensor.transpose(bX[:, c * P:(c + 1) * P], o[:, 2 * c:2 * c + 2, :]
                                                               .rearrange("p a d -> p (a d)"), ident)
                                last.then_inc(oT_mm, 1)
                            u = at(1)
                            if u:
                                pe.wait_ge(kn_ready, upto(u.g))
                                for k, (free, done) in enumerate(((qT_ready, qT_mm), (kb_ready, kT_mm))):
                                    pe.wait_ge(free, upto(u.g - 1))
                                    for c in range(UP):
                                        last = nc.tensor.transpose(bT[k][:, c * P:(c + 1) * P], qkn[:, k, 2 * c:2 * c + 2, :]
                                                                   .rearrange("p a d -> p (a d)"), ident)
                                    last.then_inc(done, 1)
                            u = at(0)
                            if u:
                                h = u.half
                                pe.wait_ge(q_sq, upto(u.g))
                                project(bA[h][:, :], lambda w: w[:, 2 * INNER + h * UW:2 * INNER + (h + 1) * UW]
                                        .rearrange("p (c a d) -> p a c d", a=2, d=DH), v_mm)
                            u = at(3)
                            if u:
                                pe.wait_ge(pT_ready, upto(u.g))
                                pe.wait_ge(v2_ready[u.slot], V2_LEAD + V2_TILE * ((u.tg - u.slot) // 2 + 1))
                                pe.wait_ge(v2_tail, V2_LEAD + V2_TAIL * (u.tg + 1))
                                pe.wait_ge(o_ready, upto(u.g - 1))
                                for c in range(UP):
                                    for w in range(WINS):
                                        last = nc.tensor.matmul(
                                            bO[w * WIN:(w + 1) * WIN, c * P:(c + 1) * P], pT[:, u.half, c, w * WIN:(w + 1) * WIN],
                                            v2[:, u.slot, w, :, u.half, c * DH:(c + 1) * DH], start=True, stop=True)
                                last.then_inc(av_mm, 1)
                            u = at(4)
                            if u:
                                pe.wait_ge(oT_ready, upto(u.g))
                                if u.half == 0:
                                    pe.wait_ge(y_used, upto(u.tg - 1))
                                    if at(7):
                                        pe.wait_ge(f1_tok, upto(at(7).tg))
                                for c in range(UP):
                                    last = nc.tensor.matmul(bY[:, 0:P], wo_sb[:, u.half * UP + c, :], oT[:, u.half, c, :],
                                                            start=(u.half == 0 and c == 0), stop=(u.half == 1 and c == UP - 1))
                                last.then_inc(y_mm, 1)
                            u = at(1)
                            if u:
                                pe.wait_ge(qT_ready, upto(u.g))
                                pe.wait_ge(kb_ready, upto(u.g))
                                pe.wait_ge(sub_done, upto(u.g - 1))
                                later = (u.tile % BT + BT - 1) // BT
                                nc.tensor.matmul(bS[:, :], identb[:, :], mask[:, ds(later * UW, UW)], start=True, stop=True)
                                for c in range(UP):
                                    for w in range(WINS):
                                        last = nc.tensor.matmul(
                                            bS[w * WIN:(w + 1) * WIN, c * P:(c + 1) * P], qT[:, c, w * WIN:(w + 1) * WIN],
                                            kb[:, u.half, c, :, w * WIN:w * WIN + 2 * WIN], start=False,
                                            stop=True, skip_group_check=True)
                                last.then_inc(s_mm, 1)
                            u = at(2)
                            if u:
                                pe.wait_ge(e_ready, upto(u.g))
                                pe.wait_ge(oT_ready, upto(u.g - 2))
                                for c in range(UP):
                                    last = nc.tensor.transpose(bX[:, c * P:(c + 1) * P], e[:, u.half, 2 * c:2 * c + 2, :]
                                                               .rearrange("p a d -> p (a d)"), ident)
                                last.then_inc(pT_mm, 1)
                        run_steps(pe, layer, step, UNITS, ATT_LAG, 4, 2)

            with ExitStack() as scope:
                xn = sb("xn", [P, 2, 4, D], scope=scope)
                xnT = sb("xnT", [P, CHUNK], scope=scope)
                xnT_hi = sb("xnT_hi", [P, 2, CHUNK], part, scope=scope)
                xnT_lo = sb("xnT_lo", [P, CHUNK], part, scope=scope)
                w1_hi, w1_lo = (sb(n, [P, 2 * FF], part, scope=scope) for n in ("w1_hi", "w1_lo"))
                ge = sb("ge", [P, 2, CHUNK], scope=scope)
                hb = sb("hb", [P, 2, FK, CHUNK], scope=scope)
                stage = sb("stage", [P, 3 * INNER], scope=scope)
                bN, bG, bV, bY = bank[0:2], bank[2:4], bank[4:6], bank[6:8]

                with nc.Block() as block:
                    @block.sync
                    def _(sp):
                        load_att_weights(sp, stage, (layer + 1) % DEPTH)

                    @block.gpsimd
                    def _(pool):
                        pool.wait_ge(w_ffn, 48 * layer + 48)
                        pool.wait_ge(w1_high, layer + 1)
                        nc.gpsimd.tensor_tensor(w1_lo[:, :], w1_sb[:, :], w1_hi[:, :], ALU.subtract).then_inc(w1_low, 1)
                        make_tables(pool, (layer + 1) % DEPTH, f_tab)
                        pool.wait_ge(w_att, 32 * layer + 64)
                        pool.sem_inc(split_turn, 1)
                        nc.gpsimd.tensor_copy(wqkv_hi[:, :], stage[:, :]).then_inc(w_split, 1)
                        pool.wait_ge(w_split, layer + 2)
                        nc.gpsimd.tensor_tensor(wqkv_lo[:, :], stage[:, :], wqkv_hi[:, :], ALU.subtract)

                    @block.vector
                    def _(dve):
                        def step(at):
                            u = at(2)
                            if u:
                                for k in range(FK):
                                    n, b = FROWS[k], (u.slot * FK + k) % 2
                                    dve.wait_ge(f2_gelu, FLEAD + FK * u.g + k + 1)
                                    dve.wait_ge(f2_val, FLEAD + FK * u.g + k + 1)
                                    dve.wait_ge(f2_y, upto(u.g - 2))
                                    nc.vector.scalar_tensor_tensor(
                                        out=hb[0:n, u.slot, k, :], in0=bV[b][0:n, :], scalar=par[0:n, B_VAL + k:B_VAL + k + 1],
                                        in1=ge[0:n, b, :], op0=ALU.add, op1=ALU.mult).then_inc(f2_h, 1)
                            u = at(0)
                            if u:
                                dve.wait_ge(f2_tr, upto(u.g - 2))
                                for j in range(4):
                                    t = u.tile * 4 + j
                                    last = nc.vector.tensor_scalar(xn[:, u.slot, j, :], xt[:, ds(t, 1), :].rearrange("p a b -> p (a b)"),
                                                                   small[:, 0, ds(t, 1)], small[:, 4, ds(t, 1)],
                                                                   ALU.subtract, ALU.mult)
                                last.then_inc(f2_norm, 1)
                            u = at(1)
                            if u:
                                dve.wait_ge(f2_val, FLEAD + FK * u.g)
                                dve.wait_ge(f2_xT, upto(u.g))
                                nc.vector.tensor_tensor(xnT_lo[:, :], xnT[:, :], xnT_hi[:, u.slot, :],
                                                        ALU.subtract).then_inc(f2_low, 1)
                            u = at(3)
                            if u:
                                dve.wait_ge(f2_y, upto(u.g))
                                c = u.tile * CHUNK + u.tile // (CHUNKS // BATCH) + 1
                                nc.vector.scalar_tensor_tensor(
                                    out=xa[:, ds(c, CHUNK)], in0=bY[u.slot][:, :], scalar=par[:, B_B2:B_B2 + 1],
                                    in1=xa[:, ds(c, CHUNK)], op0=ALU.add, op1=ALU.add).then_inc(f2_res, 1)
                        run_steps(dve, layer, step, CHUNKS, FFN_LAG, 2, 1)

                    @block.scalar
                    def _(act):
                        def step(at):
                            u = at(1)
                            if u:
                                act.wait_ge(f2_tr, upto(u.g))
                                act.wait_ge(f2_low, upto(u.g - 1))
                                nc.scalar.activation(xnT[:, :], bN[u.slot][:, :], ACT.Identity,
                                                     scale=par[:, B_G:B_G + 1], bias=par[:, B_B:B_B + 1])
                                act.wait_ge(f2_val, FLEAD + FK * (u.g - 1))
                                nc.scalar.activation(xnT_hi[:, u.slot, :], bN[u.slot][:, :], ACT.Identity,
                                                     scale=par[:, B_G:B_G + 1], bias=par[:, B_B:B_B + 1]).then_inc(f2_xT, 1)
                            u = at(2)
                            if u:
                                for k in range(FK):
                                    n, b = FROWS[k], (u.slot * FK + k) % 2
                                    act.wait_ge(f2_gate, FLEAD + FK * u.g + k + 1)
                                    act.wait_ge(f2_h, FLEAD + FK * u.g + k - 1)
                                    nc.scalar.activation(ge[0:n, b, :], bG[b][0:n, :], ACT.Gelu,
                                                         bias=par[0:n, B_GATE + k:B_GATE + k + 1]).then_inc(f2_gelu, 1)
                        act.wait_ge(w_ffn, 48 * layer + 48)
                        nc.scalar.copy(w1_hi[:, :], w1_sb[:, :]).then_inc(w1_high, 1)
                        run_steps(act, layer, step, CHUNKS, FFN_LAG, 2, 1)

                    @block.tensor
                    def _(pe):
                        def up(dst, c, n, slot, count):
                            nc.tensor.matmul(dst[0:n, :], w1_hi[:, c:c + n], xnT_hi[:, slot, :], start=True, stop=False)
                            nc.tensor.matmul(dst[0:n, :], w1_hi[:, c:c + n], xnT_lo[:, :], start=False, stop=False)
                            nc.tensor.matmul(dst[0:n, :], w1_lo[:, c:c + n], xnT_hi[:, slot, :], start=False,
                                             stop=True).then_inc(count, 1)

                        def step(at):
                            u = at(3)
                            if u:
                                pe.wait_ge(f2_res, upto(u.g - 2))
                                for k in range(FK):
                                    pe.wait_ge(f2_h, FLEAD + FK * u.g + k + 1)
                                    last = nc.tensor.matmul(bY[u.slot][:, :], w2_sb[0:FROWS[k], k, :], hb[0:FROWS[k], u.slot, k, :],
                                                            start=(k == 0), stop=(k == FK - 1))
                                last.then_inc(f2_y, 1)
                            u = at(1)
                            if u:
                                pe.wait_ge(f2_norm, upto(u.g))
                                pe.wait_ge(f2_xT, upto(u.g - 2))
                                for j in range(4):
                                    last = nc.tensor.transpose(bN[u.slot][:, j * P:(j + 1) * P], xn[:, u.slot, j, :], ident)
                                last.then_inc(f2_tr, 1)
                            u = at(2)
                            if u:
                                pe.wait_ge(w_ffn, 48 * layer + 48)
                                pe.wait_ge(w1_low, layer + 1)
                                pe.wait_ge(f2_low, upto(u.g))
                                for k in range(FK):
                                    n, b = FROWS[k], (u.slot * FK + k) % 2
                                    pe.wait_ge(f2_gelu, FLEAD + FK * u.g + k - 1)
                                    up(bG[b], FF + k * P, n, u.slot, f2_gate)
                                    pe.wait_ge(f2_h, FLEAD + FK * u.g + k - 1)
                                    up(bV[b], k * P, n, u.slot, f2_val)
                        run_steps(pe, layer, step, CHUNKS, FFN_LAG, 2, 1)

        with ExitStack() as scope:
            att = sb("att", [P, TILES, D], scope=scope)
            xf = sb("xf_end", [P, 2, P], scope=scope)
            GROUP = 8
            with nc.Block() as block:
                @block.sync
                def _(sp):
                    sp.dma_start(att[:, :, :], att_out.rearrange("(n p) d -> p n d", p=P)).then_inc(fin_in, 16)
                    dst = out.rearrange("b (n p) d -> p (b n) d", p=P)
                    for n in range(TILES // GROUP):
                        sp.wait_ge(fin_add, 1 + GROUP * (n + 1))
                        sp.dma_start(dst[:, n * GROUP:(n + 1) * GROUP, :], att[:, n * GROUP:(n + 1) * GROUP, :])\
                            .then_inc(fin_out, 16)
                    sp.wait_ge(w_att, 32 * (DEPTH + 1))
                    sp.wait_ge(fin_out, 16 * (TILES // GROUP))

                @block.gpsimd
                def _(pool):
                    with pool.Fori(0, TILES // 2) as i:
                        for e in range(2):
                            t = 2 * i + e
                            pool.wait_ge(fin_mm, 1 + 2 * i)
                            nc.gpsimd.tensor_copy(xf[:, e, :], xa[:, ds(col(t), P)]).then_inc(fin_x, 1)

                @block.tensor
                def _(pe):
                    with pe.Fori(0, TILES // 2) as i:
                        for e in range(2):
                            t = 2 * i + e
                            pe.wait_ge(fin_x, t + 1)
                            pe.wait_ge(fin_add, 1 + 2 * i)
                            nc.tensor.transpose(bank[e][:, 0:P], xf[:, e, :], ident).then_inc(fin_mm, 1)

                @block.vector
                def _(dve):
                    dve.wait_ge(fin_in, 16)
                    with dve.Fori(0, TILES // 2) as i:
                        for e in range(2):
                            t = 2 * i + e
                            dve.wait_ge(fin_mm, t + 2)
                            a = att[:, ds(t, 1), :].rearrange("p a b -> p (a b)")
                            nc.vector.tensor_tensor(a, bank[e][:, 0:P], a, ALU.add).then_inc(fin_add, 1)


_INS = ["L0_attn_hidden_states", "L0_attn_Wqkv", "L0_attn_bqkv", "L0_attn_Wout", "L0_attn_bout", "L0_ffn_Wqkv",
        "L0_ffn_q_scale", "L0_ffn_k_scale", "L0_ffn_Wo", "L0_ffn_ln_g", "L0_ffn_ln_b", "L0_ffn_W1", "L0_ffn_b1",
        "L0_ffn_W2", "L0_ffn_b2"]


def kernel(**inputs):
    import concourse.bacc as bacc
    from concourse.bass_utils import run_bass_kernel_spmd

    nc = bacc.Bacc("TRN2", target_bir_lowering=False, num_devices=1)
    arrays, args = {}, []
    for name, a in [(n, np.ascontiguousarray(inputs[n])) for n in _INS] + [("constants", constants())]:
        arrays[f"in_{name}"] = a
        args.append(nc.dram_tensor(f"in_{name}", a.shape, mybir.dt.from_np(a.dtype), kind="ExternalInput").ap())
    args.append(nc.dram_tensor("out_x", (BATCH, SEQ, D), mybir.dt.float32, kind="ExternalOutput").ap())
    program(nc, *args)
    r = run_bass_kernel_spmd(nc, [arrays], core_ids=[0])
    return r.results[0]["out_x"]
```
